# Optimizing a Trainium2 kernel written in Bass

```python
import numpy as np
import jax
import jax.numpy as jnp

def _softmax(x, axis=-1):
    return jax.nn.softmax(x, axis=axis)

def _gelu(x):
    return jax.nn.gelu(x, approximate=True)

def _silu(x):
    return jax.nn.silu(x)

def _sigmoid(x):
    return jax.nn.sigmoid(x)

def _layernorm(x, axis=-1, eps=1e-05):
    m = jnp.mean(x, axis=axis, keepdims=True)
    v = jnp.var(x, axis=axis, keepdims=True)
    return (x - m) / jnp.sqrt(v + eps)

def _scatter_add(tgt, idx, src, axis=0):
    return tgt.at[idx].add(src)

def _segment_sum(src, seg, n):
    return jax.ops.segment_sum(src, seg, n)
kernel_name = 'mk_seq_postln_d1_jaxref_r8_668b85'

def setup_inputs(seed: int=0):
    np.random.seed(seed)
    _w = jnp.asarray

    def _L0_attn_setup():
        import jax, jax.numpy as jnp
        import numpy as np
        D_MODEL = 128
        NUM_HEADS = 16
        D_K = D_MODEL // NUM_HEADS
        THETA = 10000.0
        BATCH = 2
        SEQ = 256

        def _apply_rope(x):
            S = x.shape[2]
            inv_freq = 1.0 / THETA ** (jnp.arange(0, D_K, 2, dtype=jnp.float32) / D_K)
            angles = jnp.arange(S, dtype=jnp.float32)[:, None] * inv_freq
            cos, sin = (jnp.cos(angles), jnp.sin(angles))
            x1, x2 = (x[..., ::2], x[..., 1::2])
            r1 = x1 * cos - x2 * sin
            r2 = x1 * sin + x2 * cos
            return jnp.stack([r1, r2], axis=-1).reshape(x.shape)
        key = jax.random.key(seed)
        ks = jax.random.split(key, 5)
        scale = 1.0 / np.sqrt(D_MODEL)
        return {'x': jax.random.normal(ks[0], (BATCH, SEQ, D_MODEL), dtype=jnp.float32), 'q_proj_weight': jax.random.normal(ks[1], (D_MODEL, D_MODEL), dtype=jnp.float32) * scale, 'k_proj_weight': jax.random.normal(ks[2], (D_MODEL, D_MODEL), dtype=jnp.float32) * scale, 'v_proj_weight': jax.random.normal(ks[3], (D_MODEL, D_MODEL), dtype=jnp.float32) * scale, 'o_proj_weight': jax.random.normal(ks[4], (D_MODEL, D_MODEL), dtype=jnp.float32) * scale}
    _L0_attn_in = _L0_attn_setup()

    def _L0_ffn_setup():
        import jax, jax.numpy as jnp
        import numpy as np
        B, N, D, H, E = (4, 128, 128, 16, 8)
        DK = D // H
        HID = 4 * D
        EPS = 1e-05

        def _layernorm(x, w, b):
            m = jnp.mean(x, axis=-1, keepdims=True)
            v = jnp.mean(jnp.square(x - m), axis=-1, keepdims=True)
            return (x - m) * jax.lax.rsqrt(v + EPS) * w + b

        def _msa(x, w_qkv, w_proj):
            b, n, d = x.shape
            qkv = (x @ w_qkv).reshape(b, n, 3, H, DK)
            q = qkv[:, :, 0].transpose(0, 2, 1, 3)
            k = qkv[:, :, 1].transpose(0, 2, 1, 3)
            v = qkv[:, :, 2].transpose(0, 2, 1, 3)
            attn = jnp.einsum('bhnd,bhmd->bhnm', q, k) * (1.0 / np.sqrt(DK))
            attn = jax.nn.softmax(attn, axis=-1)
            y = jnp.einsum('bhnm,bhmd->bhnd', attn, v)
            y = y.transpose(0, 2, 1, 3).reshape(b, n, d)
            return y @ w_proj

        def _moe_mlp(x, gate_w, gate_b, w1, w2):
            b, n, d = x.shape
            xf = x.reshape(b * n, d)
            logits = xf @ gate_w + gate_b
            one_hot = jax.nn.one_hot(jnp.argmax(logits, axis=-1), E, dtype=xf.dtype)
            h = jax.nn.gelu(jnp.einsum('td,edh->teh', xf, w1), approximate=True)
            y = jnp.einsum('teh,ehd->ted', h, w2)
            out = jnp.einsum('te,ted->td', one_hot, y)
            return out.reshape(b, n, d)
        key = jax.random.key(seed)
        ks = jax.random.split(key, 8)
        s = 0.02
        return {'x': jax.random.normal(ks[0], (B, N, D), jnp.float32), 'ln1_w': jnp.ones((D,), jnp.float32), 'ln1_b': jnp.zeros((D,), jnp.float32), 'w_qkv': jax.random.normal(ks[1], (D, 3 * D), jnp.float32) * s, 'w_proj': jax.random.normal(ks[2], (D, D), jnp.float32) * s, 'ln2_w': jnp.ones((D,), jnp.float32), 'ln2_b': jnp.zeros((D,), jnp.float32), 'gate_w': jax.random.normal(ks[3], (D, E), jnp.float32) * s, 'gate_b': jnp.zeros((E,), jnp.float32), 'w1': jax.random.normal(ks[4], (E, D, HID), jnp.float32) * s, 'w2': jax.random.normal(ks[5], (E, HID, D), jnp.float32) * s}
    _L0_ffn_in = _L0_ffn_setup()
    _d = {'L0_attn_x': _L0_attn_in['x'], 'L0_attn_q_proj_weight': _L0_attn_in['q_proj_weight'], 'L0_attn_k_proj_weight': _L0_attn_in['k_proj_weight'], 'L0_attn_v_proj_weight': _L0_attn_in['v_proj_weight'], 'L0_attn_o_proj_weight': _L0_attn_in['o_proj_weight'], 'L0_ffn_ln1_w': _L0_ffn_in['ln1_w'], 'L0_ffn_ln1_b': _L0_ffn_in['ln1_b'], 'L0_ffn_w_qkv': _L0_ffn_in['w_qkv'], 'L0_ffn_w_proj': _L0_ffn_in['w_proj'], 'L0_ffn_ln2_w': _L0_ffn_in['ln2_w'], 'L0_ffn_ln2_b': _L0_ffn_in['ln2_b'], 'L0_ffn_gate_w': _L0_ffn_in['gate_w'], 'L0_ffn_gate_b': _L0_ffn_in['gate_b'], 'L0_ffn_w1': _L0_ffn_in['w1'], 'L0_ffn_w2': _L0_ffn_in['w2']}
    _x0 = _d['L0_attn_x']
    _d['L0_attn_x'] = jax.random.normal(jax.random.fold_in(jax.random.key(seed), 1), (1, 2048, 128), dtype=_x0.dtype)
    del _x0
    return _d

def reference(L0_attn_x, L0_attn_q_proj_weight, L0_attn_k_proj_weight, L0_attn_v_proj_weight, L0_attn_o_proj_weight, L0_ffn_ln1_w, L0_ffn_ln1_b, L0_ffn_w_qkv, L0_ffn_w_proj, L0_ffn_ln2_w, L0_ffn_ln2_b, L0_ffn_gate_w, L0_ffn_gate_b, L0_ffn_w1, L0_ffn_w2):

    def _L0_attn_ref(x, q_proj_weight, k_proj_weight, v_proj_weight, o_proj_weight):
        import jax, jax.numpy as jnp
        import numpy as np
        D_MODEL = 128
        NUM_HEADS = 16
        D_K = D_MODEL // NUM_HEADS
        THETA = 10000.0
        BATCH = 2
        SEQ = 256

        def _apply_rope(x):
            S = x.shape[2]
            inv_freq = 1.0 / THETA ** (jnp.arange(0, D_K, 2, dtype=jnp.float32) / D_K)
            angles = jnp.arange(S, dtype=jnp.float32)[:, None] * inv_freq
            cos, sin = (jnp.cos(angles), jnp.sin(angles))
            x1, x2 = (x[..., ::2], x[..., 1::2])
            r1 = x1 * cos - x2 * sin
            r2 = x1 * sin + x2 * cos
            return jnp.stack([r1, r2], axis=-1).reshape(x.shape)
        B, S, D = x.shape
        Q = (x @ q_proj_weight.T).reshape(B, S, NUM_HEADS, D_K).transpose(0, 2, 1, 3)
        K = (x @ k_proj_weight.T).reshape(B, S, NUM_HEADS, D_K).transpose(0, 2, 1, 3)
        V = (x @ v_proj_weight.T).reshape(B, S, NUM_HEADS, D_K).transpose(0, 2, 1, 3)
        Q = _apply_rope(Q)
        K = _apply_rope(K)
        scores = jnp.einsum('bhqd,bhkd->bhqk', Q, K) / jnp.sqrt(jnp.float32(D_K))
        causal = jnp.tril(jnp.ones((S, S), dtype=bool))
        scores = jnp.where(causal, scores, -jnp.inf)
        attn = jax.nn.softmax(scores, axis=-1)
        out = jnp.einsum('bhqk,bhkd->bhqd', attn, V)
        out = out.transpose(0, 2, 1, 3).reshape(B, S, D)
        return out @ o_proj_weight.T

    def _L0_ffn_ref(x, ln1_w, ln1_b, w_qkv, w_proj, ln2_w, ln2_b, gate_w, gate_b, w1, w2):
        import jax, jax.numpy as jnp
        import numpy as np
        B, N, D, H, E = (4, 128, 128, 16, 8)
        DK = D // H
        HID = 4 * D
        EPS = 1e-05

        def _layernorm(x, w, b):
            m = jnp.mean(x, axis=-1, keepdims=True)
            v = jnp.mean(jnp.square(x - m), axis=-1, keepdims=True)
            return (x - m) * jax.lax.rsqrt(v + EPS) * w + b

        def _msa(x, w_qkv, w_proj):
            b, n, d = x.shape
            qkv = (x @ w_qkv).reshape(b, n, 3, H, DK)
            q = qkv[:, :, 0].transpose(0, 2, 1, 3)
            k = qkv[:, :, 1].transpose(0, 2, 1, 3)
            v = qkv[:, :, 2].transpose(0, 2, 1, 3)
            attn = jnp.einsum('bhnd,bhmd->bhnm', q, k) * (1.0 / np.sqrt(DK))
            attn = jax.nn.softmax(attn, axis=-1)
            y = jnp.einsum('bhnm,bhmd->bhnd', attn, v)
            y = y.transpose(0, 2, 1, 3).reshape(b, n, d)
            return y @ w_proj

        def _moe_mlp(x, gate_w, gate_b, w1, w2):
            b, n, d = x.shape
            xf = x.reshape(b * n, d)
            logits = xf @ gate_w + gate_b
            one_hot = jax.nn.one_hot(jnp.argmax(logits, axis=-1), E, dtype=xf.dtype)
            h = jax.nn.gelu(jnp.einsum('td,edh->teh', xf, w1), approximate=True)
            y = jnp.einsum('teh,ehd->ted', h, w2)
            out = jnp.einsum('te,ted->td', one_hot, y)
            return out.reshape(b, n, d)
        x = x + _msa(_layernorm(x, ln1_w, ln1_b), w_qkv, w_proj)
        x = x + _moe_mlp(_layernorm(x, ln2_w, ln2_b), gate_w, gate_b, w1, w2)
        return x
    x = L0_attn_x
    x = _layernorm(x + _L0_attn_ref(x, L0_attn_q_proj_weight, L0_attn_k_proj_weight, L0_attn_v_proj_weight, L0_attn_o_proj_weight), axis=-1)
    x = _layernorm(x + _L0_ffn_ref(x, L0_ffn_ln1_w, L0_ffn_ln1_b, L0_ffn_w_qkv, L0_ffn_w_proj, L0_ffn_ln2_w, L0_ffn_ln2_b, L0_ffn_gate_w, L0_ffn_gate_b, L0_ffn_w1, L0_ffn_w2), axis=-1)
    return x

_drawn_inputs = setup_inputs


def setup_inputs(seed=0):
    import zlib

    import numpy as np

    out = dict(_drawn_inputs(seed))
    spreads = {'L0_ffn_ln1_w': (1.0, 0.6),
     'L0_ffn_ln1_b': (0.0, 0.8),
     'L0_ffn_ln2_w': (1.0, 0.6),
     'L0_ffn_ln2_b': (0.0, 2.0),
     'L0_ffn_gate_b': (0.0, 1.297)}
    factors = {'L0_ffn_w_qkv': 8.0,
     'L0_ffn_w_proj': 8.0,
     'L0_ffn_gate_w': 3.444,
     'L0_ffn_w1': 2.791,
     'L0_ffn_w2': 2.764}
    for name, (base, spread) in spreads.items():
        noise = np.random.default_rng([zlib.crc32(name.encode()), seed]).standard_normal(out[name].shape)
        drawn = base * np.exp(spread * noise) if base else spread * noise
        out[name] = jnp.asarray(drawn.astype(out[name].dtype))
    for name, factor in factors.items():
        out[name] = (out[name] * factor).astype(out[name].dtype)
    return out
```

```python
from contextlib import ExitStack

import numpy as np

import concourse.bass as bass
from concourse import mybir

ALU = mybir.AluOpType
ACT = mybir.ActivationFunctionType
AX = mybir.AxisListType
F32 = mybir.dt.float32
BF16 = mybir.dt.bfloat16
U32 = mybir.dt.uint32
I32 = mybir.dt.int32

S = 2048
D = 128
H = 16
DK = D // H
E = 8
HID = 4 * D
EPS = 1e-5
THETA = 10000.0
P = 128

NP = 3
ROWS = NP * NP * DK
SHIFT_ROW = 96
KR = SHIFT_ROW + 1
BLK = 512
NB = S // BLK
TB = BLK // P
G = 4
HG = H // G
SCALE = float(1.0 / np.sqrt(DK))
VW = DK + 1
NSUB = 64
RING = 4

UNDER = 64.0 / SCALE
SPAN = 124.0 / SCALE


def steps_of(causal, qb):
    return TB * (qb + 1) if causal else S // P


def first_step(causal, qb):
    return sum(G * steps_of(causal, b) for b in range(qb))


def build(nc, xT_d, x_d, wa_d, wo_d, wqkv_d, wproj_d, ln1w_d, ln1b_d, ln2w_d, ln2b_d, gw_d, gb_d,
          w1_d, w2_d, cos_d, sin_d, ident_d, blk_d, esel_d, cmask_d, iota_d, out_d):
    ctx = ExitStack()
    with ctx:
        def sb(name, shape, dt=F32):
            return ctx.enter_context(nc.sbuf_tensor(name, shape, dt))

        def sem(name):
            return ctx.enter_context(nc.semaphore(name))

        KA = sb("keys_rows", [P, H * S], BF16)
        QA = sb("query_rows", [P, 2 * H * BLK], BF16)
        q3 = sb("q_parts", [P, NP, S], BF16)
        k3 = sb("k_parts", [P, 2, NP, BLK], BF16)
        V = sb("values", [P, (S // P) * H * VW])
        vring = sb("values_ring", [P, RING, HG, 32])
        Pr = sb("probs", [P, 2, HG, BLK])
        xn = sb("x_rows", [P, S // P, D])
        xT = sb("x_cols", [P, S])
        wa = sb("w_attn1", [P, 5 * D])
        wo = sb("w_out1", [P, D])
        wqkv = sb("w_attn2", [P, 3 * D])
        wproj = sb("w_out2", [P, D])
        cos = sb("cos", [P, S])
        sin = sb("sin", [P, S])
        qa = sb("q_work", [P, BLK])
        qb_ = sb("q_work2", [P, BLK])
        ka = sb("k_work", [P, BLK])
        kb_ = sb("k_work2", [P, BLK])
        sq = sb("squares", [P, 3, BLK], BF16)
        accs, attT = qb_, kb_
        zb = sb("z_rows", [P, TB, D])
        att = sb("attn_rows", [P, TB, D])
        ident = sb("ident", [P, P])
        blkf = sb("blk_f", [P, H])
        blk = sb("blk", [P, H], BF16)
        cmask = sb("cmask", [P, P])
        masked = sb("masked", [P, P])
        ln = sb("ln_wb", [P, 4])
        gw = sb("gate_w", [P, E])
        gb = sb("gate_b", [P, E])
        iota = sb("iota", [P, E])
        kblk = sb("k_blockdiag", [P, H * NSUB], BF16)
        rec = sb("recip", [P, TB, HG])
        mnat = sb("row_max", [P, TB, H])
        mpart = sb("row_max_parts", [P, 2])
        lnat = sb("row_low", [P, S // P, H])
        nq2 = sb("q_norms", [H, S], BF16)
        kmx = sb("k_norm_max", [H, 4])
        oks = sb("row_ok", [H, 4])
        negc = sb("neg_shift", [H, S], BF16)
        negf = sb("neg_shift_final", [H, BLK], BF16)
        ones16 = sb("ones16", [H, 1])
        flags = sb("flags", [1, 2 * NB], I32)
        st = sb("ln_stats", [P, TB, 6])
        mv = sb("ln_meanvar", [P, TB, 2])
        nw = sb("ln_newton", [P, 4, TB])

        kaf, qaf = KA[:, :].bitcast(F32), QA[:, :].bitcast(F32)
        w1s = kaf[:, 0:E * HID].rearrange("p (e n) -> p e n", e=E)
        w2s = kaf[:, E * HID:2 * E * HID].rearrange("p (e c d) -> p e c d", e=E, c=TB)
        xe = kaf[:, 2 * E * HID:3 * E * HID].rearrange("p (e t) -> p e t", e=E)
        ms = KA[:, 6 * E * HID:7 * E * HID].rearrange("p (e t) -> p e t", e=E)
        hid = qaf[:, 0:TB * BLK].rearrange("p (c t) -> p c t", c=TB)
        he = qaf[:, TB * BLK:2 * TB * BLK].rearrange("p (c t) -> p c t", c=TB)
        lT, uT, cT = (Pr[0:H, 1, n, :] for n in (1, 2, 3))
        yb = Pr[:, 0, 0, :].rearrange("p (i d) -> p i d", i=TB)
        hT = Pr[:, 0, 1, :]
        yT = Pr[:, 0, 2, :]
        ob = Pr[:, 0, 3, :].rearrange("p (i d) -> p i d", i=TB)
        lg = Pr[:, 1, 0, 0:TB * E].rearrange("p (i e) -> p i e", i=TB)
        mx8 = Pr[:, 1, 0, 64:64 + TB * 8].rearrange("p (i e) -> p i e", i=TB)
        ix8 = Pr[:, 1, 0, 128:128 + TB * 8].bitcast(U32).rearrange("p (i e) -> p i e", i=TB)
        ixf = Pr[:, 1, 0, 192:192 + TB]
        oh = Pr[:, 1, 0, 256:256 + TB * E].rearrange("p (i e) -> p i e", i=TB)
        ohT = Pr[0:E, 1, 1, :].bitcast(BF16)[:, 0:BLK]
        eself = qaf[0:E, 6144:6144 + E * P]
        esel = QA[0:E, 14336:14336 + E * P]

        k_scratch = nc.dram_tensor("k_scratch", (2, NB, NP, DK, H, BLK), BF16, kind="Internal").ap()
        q_scratch = nc.dram_tensor("q_scratch", (2, NB, NP, DK, H, BLK), BF16, kind="Internal").ap()

        ps = ctx.enter_context(nc.psum_tensor("ps", [P, 8, BLK], F32))
        psS = ps[:, 0:4, :]
        acc = ps[:, 4, :]
        psT = ps[:, 5, :]

        ld_a, ld_w, ld_x, ld_m, ld_e = (sem(n) for n in ("ld_a", "ld_w", "ld_x", "ld_m", "ld_e"))
        ld_b = [sem(f"ld_b{b}") for b in range(NB)]
        init, scratch_out = sem("init"), sem("scratch_out")
        dch, pch = sem("dve_chain"), sem("pool_chain")
        A = {}
        for a in (1, 2):
            s = {}
            for n in ("q_proj", "k_proj", "v_proj", "q_taken", "k_taken", "v_taken", "k_mid", "q_split",
                      "k_split", "sq_q", "sq_k", "norm_mm", "norm_taken", "kmx", "root", "ok", "ok_mm", "flag",
                      "low_mm", "low_taken", "lowT", "final",
                      "S", "exp", "pv", "v", "dg", "dg_seen", "evac", "recip", "pt", "norm", "post_t", "post_e", "post_p", "post_x"):
                s[n] = sem(f"a{a}_{n}")
            for n in ("k_rows", "q_rows", "c_row", "gen_s", "gen_f"):
                s[n] = [sem(f"a{a}_{n}{b}") for b in range(NB)]
            A[a] = s
        A[2]["hT"], A[2]["zT"] = sem("a2_hT"), sem("a2_zT")
        m_z, m_zT, m_h, m_g, m_oh, m_ohT, m_ohTs = (sem(f"m_{n}") for n in ("z", "zT", "h", "g", "oh", "ohT", "ohTs"))
        m_mk, m_ms, m_xe, m_pre, m_hid, m_he, m_hd, m_yT, m_yn, m_out, m_done = (
            sem(f"m_{n}") for n in ("mk", "ms", "xe", "pre", "hid", "he", "hd", "yT", "yn", "out", "done"))

        KAv = KA[:, :].rearrange("p (h t) -> p h t", h=H)
        QAv = QA[:, :].rearrange("p (s h t) -> p s h t", s=2, h=H)
        Vv = V[:, :].rearrange("p (k h w) -> p k h w", h=H, w=VW)

        block = ctx.enter_context(nc.Block())

        @block.sync
        def _(sp):
            sp.dma_start(wa[:, :], wa_d).then_inc(ld_a, 16)
            for b in range(NB):
                c = slice(b * BLK, (b + 1) * BLK)
                sp.dma_start(xT[:, c], xT_d[:, c]).then_inc(ld_b[b], 16)
                sp.dma_start(cos[:, c], cos_d[:, c]).then_inc(ld_b[b], 16)
                sp.dma_start(sin[:, c], sin_d[:, c]).then_inc(ld_b[b], 16)
            for t, s in ((blkf, blk_d), (cmask, cmask_d), (ident, ident_d), (wo, wo_d), (wqkv, wqkv_d),
                         (wproj, wproj_d), (gw, gw_d), (iota, iota_d), (gb, gb_d)):
                sp.dma_start(t[:, :], s).then_inc(ld_w, 16)
            for n, s in enumerate((ln1w_d, ln1b_d, ln2w_d, ln2b_d)):
                sp.dma_start(ln[:, n:n + 1], s).then_inc(ld_w, 16)
            sp.dma_start(xn[:, :, :], x_d.rearrange("(t p) d -> p t d", p=P)).then_inc(ld_x, 16)

            parts_out = [0]

            def out_and_in(parts, scratch):
                sp.dma_start(scratch.rearrange("j d h t -> (d h) j t"), parts).then_inc(scratch_out, 16)
                parts_out[0] += 16
                sp.wait_ge(scratch_out, parts_out[0])
                return scratch.rearrange("j d h t -> (j d) h t")

            def key_rows(a, b):
                sp.wait_ge(A[a]["k_split"], b + 1)
                src = out_and_in(k3[:, b % 2], k_scratch[a - 1, b])
                for i in range(NP):
                    for j in range(NP):
                        r = (i * NP + j) * DK
                        sp.dma_start(KAv[r:r + DK, :, b * BLK:(b + 1) * BLK], src[i * DK:(i + 1) * DK]
                                     ).then_inc(A[a]["k_rows"][b], 16)

            def query_rows(a, b):
                sp.wait_ge(A[a]["q_split"], b + 1)
                src = out_and_in(q3[:, :, b * BLK:(b + 1) * BLK], q_scratch[a - 1, b])
                for i in range(NP):
                    r = i * NP * DK
                    sp.dma_start(QAv[r:r + NP * DK, b % 2, :, :], src).then_inc(A[a]["q_rows"][b], 16)

            def shift_row(a, b):
                sp.wait_ge(A[a]["final"], b + 1)
                sp.dma_start(QAv[SHIFT_ROW:SHIFT_ROW + 1, b % 2, :, :], negf[:, :]).then_inc(A[a]["c_row"][b], 16)

            for a in (1, 2):
                causal = a == 1
                if a == 1:
                    sp.wait_ge(init, 3)
                else:
                    sp.wait_ge(A[1]["S"], 2 * first_step(True, NB))
                for b in range(NB):
                    key_rows(a, b)
                    if b < 2:
                        query_rows(a, b)
                shift_row(a, 0)
                for b in range(1, NB):
                    if b >= 2:
                        sp.wait_ge(A[a]["S"], 2 * first_step(causal, b - 1))
                        query_rows(a, b)
                    shift_row(a, b)
            sp.wait_ge(A[2]["S"], 2 * first_step(False, NB))
            sp.dma_start(w1s, w1_d.rearrange("e p n -> p e n")).then_inc(ld_m, 16)
            sp.dma_start(w2s, w2_d.rearrange("e (c p) d -> p e c d", p=P)).then_inc(ld_m, 16)
            sp.dma_start(eself, esel_d).then_inc(ld_e, 16)
            for b in range(NB):
                sp.wait_ge(m_out, b + 1)
                sp.dma_start(out_d[b * BLK:(b + 1) * BLK, :].rearrange("(i p) d -> p i d", p=P), ob
                             ).then_inc(m_done, 16)
                sp.wait_ge(m_done, 16 * (b + 1))

        @block.tensor
        def _(pe):
            def mm(out, l, r, start=True, stop=True):
                return nc.tensor.matmul(out, l, r, start=start, stop=stop, skip_group_check=True)

            def project(a, b):
                s = A[a]
                if a == 1:
                    pe.wait_ge(ld_b[b], 48)
                    src, w = xT[:, b * BLK:(b + 1) * BLK], wa
                    cols = ((0, 0, "q_proj"), (1, 1, "q_proj"), (2, 2, "k_proj"), (3, 3, "k_proj"))
                    vcol = 4
                else:
                    pe.wait_ge(s["hT"], b + 1)
                    src, w = hT, wqkv
                    cols = ((0, 0, "q_proj"), (1, 2, "k_proj"))
                    vcol = 2
                for n, bank, done in cols:
                    pe.wait_ge(s["q_taken" if done[0] == "q" else "k_taken"], b)
                    mm(ps[:, bank, :], w[:, n * D:(n + 1) * D], src).then_inc(s[done], 1)
                pe.wait_ge(s["v_taken"], b)
                for i in range(TB):
                    last = mm(ps[:, 4, i * D:(i + 1) * D], src[:, i * P:(i + 1) * P], w[:, vcol * D:(vcol + 1) * D])
                last.then_inc(s["v_proj"], 1)

            def norms(a, b):
                s = A[a]
                if a == 1 and b == 0:
                    pe.wait_ge(init, 3)
                pe.wait_ge(s["sq_q"], b + 1)
                pe.wait_ge(s["sq_k"], b + 1)
                pe.wait_ge(s["norm_taken"], b)
                mm(ps[0:H, 5, :], blk[:, :], sq[:, 0, :])
                last = mm(ps[0:H, 6, :], blk[:, :], sq[:, 1, :])
                if a == 1:
                    last = mm(ps[0:H, 7, :], blk[:, :], sq[:, 2, :])
                last.then_inc(s["norm_mm"], 1)

            def lows(b):
                s = A[2]
                for i in range(TB):
                    t = b * TB + i
                    if t == 0:
                        pe.wait_ge(s["low_taken"], 1)
                    pe.wait_ge(s["low_taken"], t + 1)
                    for c in range(H * NSUB // BLK):
                        last = mm(ps[:, c, :], q3[:, 0, t * P:(t + 1) * P], kblk[:, c * BLK:(c + 1) * BLK])
                    last.then_inc(s["low_mm"], 1)
                pe.wait_ge(s["low_taken"], (b + 1) * TB + 1)
                pe.wait_ge(s["lowT"], 2 * b)
                for i in range(TB):
                    last = nc.tensor.transpose(ps[0:H, 7, i * P:(i + 1) * P], lnat[:, b * TB + i, :], ident[:, :])
                last.then_inc(s["lowT"], 1)

            def count_ok(a, b):
                pe.wait_ge(A[a]["ok"], b + 1)
                mm(ps[0:1, 5, 0:1], oks[:, 2:3], ones16[:, :]).then_inc(A[a]["ok_mm"], 1)

            def general(a, qb, base):
                s = A[a]
                pe.wait_ge(s["flag"], qb + 1)
                bad = pe.value_load(flags[0:1, (a - 1) * NB + qb:(a - 1) * NB + qb + 1], min_val=0, max_val=H)
                with pe.If(bad != 0):
                    for b in range(qb + 1 if a == 1 else NB):
                        pe.wait_ge(s["k_rows"][b], 16 * NP * NP)
                    pe.wait_ge(s["q_rows"][qb], 16 * NP)
                    pe.wait_ge(s["exp"], 2 * base + 2)
                    with pe.Fori(0, H) as h:
                        for i in range(TB):
                            nk = qb * BLK + (i + 1) * P if a == 1 else S
                            pe.wait_ge(s["gen_f"][qb], h * TB + i + 1)
                            for c in range(0, nk, BLK):
                                n = min(BLK, nk - c)
                                last = mm(ps[:, c // BLK, 0:n],
                                          QA[0:ROWS, bass.ds(h * BLK + (qb % 2) * H * BLK + i * P, P)],
                                          KA[0:ROWS, bass.ds(h * S + c, n)])
                            last.then_inc(s["gen_s"][qb], 1)
                    pe.wait_ge(s["gen_f"][qb], H * TB + 1)
                    for i in range(TB):
                        last = nc.tensor.transpose(ps[0:H, 7, i * P:(i + 1) * P], mnat[:, i, :], ident[:, :])
                    last.then_inc(s["gen_s"][qb], 1)

            def scores(s, slot, g, kt_at, i, t, lo):
                for p in range(2):
                    pe.wait_ge(s["exp"], 2 * t + p + 1)
                    for hh in range(2):
                        h = g * HG + 2 * p + hh
                        last = mm(ps[:, 2 * p + hh, lo:BLK], KA[0:KR, bass.ds(h * S + kt_at, P)],
                                  QA[0:KR, bass.ds(h * BLK + slot * H * BLK + lo, BLK - lo)])
                    last.then_inc(s["S"], 1)

            def values(a, i, t, lo, start, stop, n, cut=None):
                s = A[a]
                pe.wait_ge(s["v"], t + 1)
                pe.wait_ge(s["exp"], 2 * t + 4)
                if cut is not None:
                    pe.wait_ge(s["dg"], cut)
                if start:
                    pe.wait_ge(s["evac"], n)
                for hh in range(HG):
                    last = mm(acc[32 * hh:32 * hh + 32, lo:BLK], vring[:, i, hh, :], Pr[:, i % 2, hh, lo:BLK],
                              start=start, stop=stop)
                last.then_inc(s["pv"], 1)

            def turn(a, n):
                s = A[a]
                pe.wait_ge(s["evac"], n + 1)
                for i in range(TB):
                    last = nc.tensor.transpose(psT[:, i * P:(i + 1) * P], accs[:, i * P:(i + 1) * P], ident[:, :])
                last.then_inc(s["pt"], 1)

            def post_turn(a, qb):
                s = A[a]
                pe.wait_ge(s["norm"], G * (qb + 1))
                pe.wait_ge(s["post_e"], qb)
                for i in range(TB):
                    last = nc.tensor.transpose(ps[:, 6, i * P:(i + 1) * P], att[:, i, :], ident[:, :])
                last.then_inc(s["post_t"], 1)

            def post_project(a, qb):
                s = A[a]
                pe.wait_ge(s["post_e"], qb + 1)
                pe.wait_ge(s["post_x"], qb)
                for i in range(TB):
                    last = mm(ps[:, 7, i * D:(i + 1) * D], attT[:, i * P:(i + 1) * P], (wo if a == 1 else wproj)[:, :])
                last.then_inc(s["post_p"], 1)

            def group(a, qb, g, n, unrolled):
                s = A[a]
                causal = a == 1
                T = steps_of(causal, qb)
                base = first_step(causal, qb)
                t0 = base + g * T
                full = qb if causal else NB
                first = unrolled

                def block_steps(kb, diag, opening):
                    for i in range(TB):
                        lo = i * P if diag else 0
                        t = t0 + kb * TB + i
                        scores(s, qb % 2, g, kb * BLK + i * P, i, t, lo)
                        if opening and i == 0:
                            if not first:
                                values(a, TB - 1, t - 1, (TB - 1) * P if causal else 0, False, True, n,
                                       n * TB if causal else None)
                        else:
                            j = (i - 1) % TB
                            cut = diag and i > 0
                            values(a, j, t - 1, j * P if cut else 0, opening and i == 1, False, n,
                                   n * TB + i if cut else None)
                        if opening and i == 2:
                            if not first:
                                turn(a, n - 1)
                            elif qb > 0:
                                turn(a, n - 1)
                        if first and qb > 0:
                            if (kb, i) == (1, 0):
                                post_turn(a, qb - 1)
                            if (kb, i) == (1, 2):
                                post_project(a, qb - 1)

                block_steps(0, full == 0, True)
                if full > 1:
                    if unrolled:
                        for kb in range(1, full):
                            block_steps(kb, False, False)
                    else:
                        with pe.Fori(1, full) as kb:
                            block_steps(kb, False, False)
                if causal and full > 0:
                    block_steps(full, True, False)

            def attention(a):
                causal = a == 1
                s = A[a]
                general(a, 0, 0)
                for qb in range(NB):
                    base = first_step(causal, qb)
                    T = steps_of(causal, qb)
                    if causal:
                        pe.wait_ge(s["k_rows"][qb], 16 * NP * NP)
                    elif qb == 0:
                        for b in range(NB):
                            pe.wait_ge(s["k_rows"][b], 16 * NP * NP)
                    pe.wait_ge(s["q_rows"][qb], 16 * NP)
                    pe.wait_ge(s["c_row"][qb], 16)
                    group(a, qb, 0, G * qb, True)
                    if qb + 1 < NB:
                        general(a, qb + 1, base + T)
                    with pe.Fori(1, G) as g:
                        group(a, qb, g, G * qb + g, False)
                    values(a, TB - 1, base + G * T - 1, (TB - 1) * P if causal else 0, False, True, 0,
                           G * (qb + 1) * TB if causal else None)
                turn(a, G * NB - 1)
                post_turn(a, NB - 1)
                post_project(a, NB - 1)

            pe.wait_ge(ld_a, 16)
            for b in range(NB):
                project(1, b)
                norms(1, b)
                count_ok(1, b)
            attention(1)
            for b in range(NB):
                pe.wait_ge(A[2]["zT"], 2 * b + 1)
                for i in range(TB):
                    last = nc.tensor.transpose(psT[:, i * P:(i + 1) * P], zb[:, i, :], ident[:, :])
                last.then_inc(A[2]["zT"], 1)
                project(2, b)
                norms(2, b)
            for b in range(NB):
                lows(b)
                count_ok(2, b)
            attention(2)
            pe.wait_ge(ld_m, 32)
            for b in range(NB):
                pe.wait_ge(m_z, b + 1)
                for i in range(TB):
                    last = nc.tensor.transpose(psT[:, i * P:(i + 1) * P], zb[:, i, :], ident[:, :])
                last.then_inc(m_zT, 1)
                pe.wait_ge(m_h, b + 1)
                for i in range(TB):
                    last = mm(ps[:, 6, i * E:(i + 1) * E], hT[:, i * P:(i + 1) * P], gw[:, :])
                last.then_inc(m_g, 1)
                pe.wait_ge(m_oh, b + 1)
                for i in range(TB):
                    last = nc.tensor.transpose(ps[0:E, 7, i * P:(i + 1) * P], oh[:, i, :], ident[:, :])
                last.then_inc(m_ohT, 1)
                pe.wait_ge(m_ohTs, b + 1)
                for e in range(E):
                    pe.wait_ge(m_ms, b * E + max(0, e - 1))
                    mm(ps[:, 5 + e % 2, :], esel[:, e * P:(e + 1) * P], ohT).then_inc(m_mk, 1)
                for c in range(TB):
                    pe.wait_ge(m_hid, b * TB)
                    for e in range(E):
                        if c == 0:
                            pe.wait_ge(m_xe, b * E + e + 1)
                        last = mm(ps[:, c, :], w1s[:, e, c * P:(c + 1) * P], xe[:, e, :], e == 0, e == E - 1)
                    last.then_inc(m_pre, 1)
                for c in range(TB):
                    for e in range(E):
                        n = b * TB * E + c * E + e
                        pe.wait_ge(m_he, n + 1)
                        mm(ps[:, 4, :], w2s[:, e, c, :], he[:, n % TB, :], c == 0 and e == 0,
                           c == TB - 1 and e == E - 1).then_inc(m_hd, 1)
                pe.wait_ge(m_yT, b + 1)
                for i in range(TB):
                    last = nc.tensor.transpose(ps[:, 7, i * P:(i + 1) * P], yT[:, i * P:(i + 1) * P], ident[:, :])
                last.then_inc(m_yn, 1)

        @block.scalar
        def _(act):
            def taken(a, b):
                s = A[a]
                if a == 2:
                    act.wait_ge(s["k_proj"], b + 1)
                    act.wait_ge(s["k_mid"], b)
                    nc.scalar.activation(ka[:, :], ps[:, 2, :], ACT.Copy).then_inc(s["k_taken"], 1)
                act.wait_ge(s["v_proj"], b + 1)
                nc.scalar.activation(Vv[:, b * TB:(b + 1) * TB, :, 0:DK],
                                     ps[:, 4, :].rearrange("p (i h d) -> p i h d", i=TB, h=H),
                                     ACT.Copy).then_inc(s["v_taken"], 1)

            def root(a, b):
                act.wait_ge(A[a]["kmx"], b + 1)
                nc.scalar.activation(uT[:, :], nq2[:, b * BLK:(b + 1) * BLK], ACT.Sqrt,
                                     scale=kmx[:, 2:3]).then_inc(A[a]["root"], 1)

            def exps(a, qb, g, kb, diag):
                s = A[a]
                causal = a == 1
                t0 = first_step(causal, qb) + g * steps_of(causal, qb) + kb * TB
                for i in range(TB):
                    lo = i * P if diag else 0
                    t = t0 + i
                    act.wait_ge(s["pv"], t + 3)
                    for p in range(2):
                        act.wait_ge(s["S"], 2 * t + p + 1)
                        nc.scalar.activation(Pr[:, i % 2, 2 * p:2 * p + 2, lo:BLK], ps[:, 2 * p:2 * p + 2, lo:BLK],
                                             ACT.Exp, scale=SCALE).then_inc(s["exp"], 1)

            def attention(a):
                causal = a == 1
                for qb in range(NB):
                    full = qb if causal else NB
                    with act.Fori(0, G) as g:
                        if full:
                            with act.Fori(0, full) as kb:
                                exps(a, qb, g, kb, False)
                        if causal:
                            exps(a, qb, g, full, True)

            act.wait_ge(init, 3)
            for b in range(NB):
                taken(1, b)
                root(1, b)
            attention(1)
            for b in range(NB):
                taken(2, b)
            for b in range(NB):
                root(2, b)
            attention(2)
            for b in range(NB):
                for e in range(E):
                    act.wait_ge(m_mk, b * E + e + 1)
                    act.wait_ge(m_hd, b * TB * E)
                    nc.scalar.activation(ms[:, e, :], ps[:, 5 + e % 2, :], ACT.Copy).then_inc(m_ms, 1)
                for c in range(TB):
                    act.wait_ge(m_pre, b * TB + c + 1)
                    nc.scalar.activation(hid[:, c, :], ps[:, c, :], ACT.Gelu_apprx_tanh).then_inc(m_hid, 1)

        @block.gpsimd
        def _(pool):
            chain = [0]

            def link(ins):
                chain[0] += 1
                ins.then_inc(pch, 1)
                pool.wait_ge(pch, chain[0])

            def split_k(a, b):
                s = A[a]
                pool.wait_ge(s["k_taken"], b + 1)
                if b >= 2:
                    pool.wait_ge(s["k_rows"][b - 2], 16 * NP * NP)
                elif a == 2:
                    pool.wait_ge(A[1]["k_rows"][b + 2], 16 * NP * NP)
                if a == 1:
                    link(nc.gpsimd.tensor_tensor(ka[:, :], ka[:, :], kb_[:, :], ALU.add))
                kk = k3[:, b % 2]
                link(nc.gpsimd.tensor_copy(kk[:, 0, :], ka[:, :]))
                if b:
                    pool.wait_ge(s["norm_mm"], b)
                elif a == 2:
                    pool.wait_ge(A[1]["norm_mm"], NB)
                nc.gpsimd.tensor_tensor(sq[:, 1, :], ka[:, :], ka[:, :], ALU.mult).then_inc(s["sq_k"], 1)
                pool.wait_ge(s["sq_k"], b + 1)
                link(nc.gpsimd.tensor_tensor(ka[:, :], ka[:, :], kk[:, 0, :], ALU.subtract))
                link(nc.gpsimd.tensor_copy(kk[:, 1, :], ka[:, :]))
                nc.gpsimd.tensor_tensor(kk[:, 2, :], ka[:, :], kk[:, 1, :], ALU.subtract).then_inc(s["k_split"], 1)
                pool.wait_ge(s["k_split"], b + 1)
                pool.sem_inc(s["k_mid"], 1)

            def ring(a, qb, g, kb, diag):
                s = A[a]
                causal = a == 1
                t0 = first_step(causal, qb) + g * steps_of(causal, qb) + kb * TB
                for i in range(TB):
                    t = t0 + i
                    pool.wait_ge(s["pv"], t + 1)
                    nc.gpsimd.tensor_copy(
                        vring[:, i, :, 0:VW],
                        V[:, bass.ds((kb * TB + i) * H * VW + g * HG * VW, HG * VW)].rearrange("p (h w) -> p h w", h=HG)
                    ).then_inc(s["v"], 1)
                    if causal and diag:
                        pool.wait_ge(s["exp"], 2 * t + 4)
                        pool.sem_inc(s["dg_seen"], 1)
                        cut = Pr[:, i % 2, :, i * P:(i + 1) * P]
                        nc.gpsimd.affine_select(out=cut, in_=cut, compare_op=ALU.is_ge, fill=0.0, base=0,
                                                pattern=[[0, HG], [1, P]], channel_multiplier=-1).then_inc(s["dg"], 1)

            link(nc.gpsimd.memset(V[:, :], 1.0))
            link(nc.gpsimd.memset(vring[:, :, :, :], 0.0))
            nc.gpsimd.memset(qaf[64:P, :], 0.0).then_inc(init, 1)
            for a in (1, 2):
                pool.sem_inc(A[a]["pv"], RING)
                pool.sem_inc(A[a]["exp"], 2)
            for a in (1, 2):
                for b in range(NB):
                    split_k(a, b)
                causal = a == 1
                for b in range(NB):
                    pool.wait_ge(A[a]["v_taken"], b + 1)
                for qb in range(NB):
                    full = qb if causal else NB
                    with pool.Fori(0, G) as g:
                        if full:
                            with pool.Fori(0, full) as kb:
                                ring(a, qb, g, kb, False)
                        if causal:
                            ring(a, qb, g, full, True)
            for b in range(NB):
                for e in range(E):
                    pool.wait_ge(m_ms, b * E + e + 1)
                    if e == 0:
                        pool.wait_ge(m_h, b + 1)
                        pool.wait_ge(m_pre, b * TB)
                    nc.gpsimd.tensor_tensor(xe[:, e, :], hT, ms[:, e, :], ALU.mult).then_inc(m_xe, 1)

        @block.vector
        def _(dve):
            chain = [0]

            def link(ins):
                chain[0] += 1
                ins.then_inc(dch, 1)
                dve.wait_ge(dch, chain[0])

            tt, ts = nc.vector.tensor_tensor, nc.vector.tensor_scalar

            def layernorm(dst, src):
                for i in range(TB):
                    ins = nc.vector.bn_stats(st[:, i, :], src[:, i, :])
                link(ins)
                for i in range(TB):
                    ins = nc.vector.bn_aggr(mv[:, i, :], st[:, i, :])
                link(ins)
                v, y, h, t = (nw[:, n, :] for n in range(4))
                link(ts(v, mv[:, :, 1], EPS, None, ALU.add))
                link(ts(y.bitcast(I32), v.bitcast(I32), -0.5, 1597463007.0, ALU.mult, ALU.add))
                link(ts(h, v, -0.5, None, ALU.mult))
                for _ in range(4):
                    link(tt(t, y, y, ALU.mult))
                    link(tt(t, t, h, ALU.mult))
                    link(nc.vector.scalar_tensor_tensor(out=y, in0=t, scalar=1.5, in1=y, op0=ALU.add, op1=ALU.mult))
                for i in range(TB):
                    ins = ts(dst[:, i, :], src[:, i, :], mv[:, i, 0:1], nw[:, 1, i:i + 1], ALU.subtract, ALU.mult)
                return ins

            def split_q(a, b):
                s = A[a]
                c = slice(b * BLK, (b + 1) * BLK)
                if a == 1:
                    dve.wait_ge(ld_b[b], 48)
                    dve.wait_ge(s["q_proj"], 2 * b + 2)
                    tt(qa[:, :], ps[:, 0, :], cos[:, c], ALU.mult)
                    tt(qb_[:, :], ps[:, 1, :], sin[:, c], ALU.mult).then_inc(s["q_taken"], 1)
                    dve.wait_ge(s["k_proj"], 2 * b + 2)
                    dve.wait_ge(s["k_mid"], b)
                    tt(ka[:, :], ps[:, 2, :], cos[:, c], ALU.mult)
                    tt(kb_[:, :], ps[:, 3, :], sin[:, c], ALU.mult).then_inc(s["k_taken"], 1)
                    dve.wait_ge(s["q_taken"], b + 1)
                    link(tt(qa[:, :], qa[:, :], qb_[:, :], ALU.add))
                else:
                    dve.wait_ge(s["q_proj"], b + 1)
                    nc.vector.tensor_copy(qa[:, :], ps[:, 0, :]).then_inc(s["q_taken"], 1)
                    dve.wait_ge(s["q_taken"], b + 1)
                link(nc.vector.tensor_copy(q3[:, 0, c], qa[:, :]))
                if b:
                    dve.wait_ge(s["norm_mm"], b)
                elif a == 2:
                    dve.wait_ge(A[1]["norm_mm"], NB)
                link(tt(sq[:, 0, :], qa[:, :], qa[:, :], ALU.mult))
                link(tt(qa[:, :], qa[:, :], q3[:, 0, c], ALU.subtract))
                link(nc.vector.tensor_copy(q3[:, 1, c], qa[:, :]))
                tt(q3[:, 2, c], qa[:, :], q3[:, 1, c], ALU.subtract).then_inc(s["q_split"], 1)
                dve.wait_ge(s["k_split"], b + 1)
                if a == 1:
                    tt(sq[:, 2, :], q3[:, 0, c], k3[:, b % 2, 0, :], ALU.mult).then_inc(s["sq_q"], 1)
                else:
                    if b == 0:
                        tt(kblk[:, :].rearrange("p (h t) -> p h t", h=H),
                           k3[:, 0, 0, 0:NSUB].unsqueeze(1).to_broadcast([P, H, NSUB]),
                           blk[:, :].unsqueeze(2).to_broadcast([P, H, NSUB]), ALU.mult).then_inc(s["low_taken"], 1)
                    nc.vector.tensor_copy(oks[:, 3:4], ones16[:, :]).then_inc(s["sq_q"], 1)

            def take_norms(a, b):
                s = A[a]
                c = slice(b * BLK, (b + 1) * BLK)
                dve.wait_ge(s["norm_mm"], b + 1)
                if b:
                    dve.wait_ge(s["root"], b) if a == 1 else None
                nc.vector.tensor_copy(nq2[:, c], ps[0:H, 5, :])
                link(nc.vector.tensor_reduce(kmx[:, 1 if b else 0:2 if b else 1], ps[0:H, 6, :], AX.X, ALU.max))
                if b:
                    link(tt(kmx[:, 0:1], kmx[:, 0:1], kmx[:, 1:2], ALU.max))
                if a == 1:
                    link(nc.vector.tensor_copy(lT[:, :], ps[0:H, 7, :]))
                ins = ts(kmx[:, 2:3], kmx[:, 0:1], 1.03, 1e-20, ALU.mult, ALU.add)
                ins.then_inc(s["norm_taken"], 1)
                dve.wait_ge(s["norm_taken"], b + 1)

            def shift(a, b):
                s = A[a]
                c = slice(b * BLK, (b + 1) * BLK)
                dve.sem_inc(s["kmx"], 1)
                dve.wait_ge(s["root"], b + 1)
                link(nc.vector.scalar_tensor_tensor(out=cT[:, :], in0=uT[:, :], scalar=-UNDER, in1=lT[:, :],
                                                    op0=ALU.add, op1=ALU.max))
                link(ts(negc[:, c], cT[:, :], -1.0, None, ALU.mult))
                link(tt(uT[:, :], uT[:, :], lT[:, :], ALU.subtract))
                link(nc.vector.scalar_tensor_tensor(out=cT[:, :], in0=nq2[:, c], scalar=1e-10, in1=uT[:, :],
                                                    op0=ALU.mult, op1=ALU.max))
                link(ts(kmx[:, 3:4], kmx[:, 0:1], 1e-10, None, ALU.mult))
                link(ts(cT[:, :], cT[:, :], kmx[:, 3:4], SPAN, ALU.max, ALU.is_le))
                link(nc.vector.tensor_reduce(oks[:, 0:1], cT[:, :], AX.X, ALU.min))
                ts(oks[:, 2:3], oks[:, 0:1], -1.0, 1.0, ALU.mult, ALU.add).then_inc(s["ok"], 1)
                dve.wait_ge(s["ok_mm"], b + 1)
                nc.vector.tensor_copy(flags[0:1, (a - 1) * NB + b:(a - 1) * NB + b + 1], ps[0:1, 5, 0:1]
                                      ).then_inc(s["flag"], 1)

            def lows(b):
                s = A[2]
                for i in range(TB):
                    t = b * TB + i
                    dve.wait_ge(s["low_mm"], t + 1)
                    nc.vector.tensor_reduce(lnat[:, t, :],
                                            ps[:, 0:2, :].rearrange("p b (h t) -> p (b h) t", t=NSUB),
                                            AX.X, ALU.max).then_inc(s["low_taken"], 1)
                dve.wait_ge(s["lowT"], 2 * b + 1)
                nc.vector.tensor_copy(lT[:, :], ps[0:H, 7, :]).then_inc(s["lowT"], 1)
                dve.wait_ge(s["lowT"], 2 * b + 2)

            def general(a, qb):
                s = A[a]
                dve.wait_ge(s["flag"], qb + 1)
                if qb:
                    dve.wait_ge(s["c_row"][qb - 1], 16)
                bad = dve.value_load(flags[0:1, (a - 1) * NB + qb:(a - 1) * NB + qb + 1], min_val=0, max_val=H)
                with dve.If(bad != 0):
                    dve.sem_inc(s["gen_f"][qb], 1)
                    with dve.Fori(0, H) as h:
                        for i in range(TB):
                            dve.wait_ge(s["gen_s"][qb], h * TB + i + 1)
                            to = mnat[:, i, bass.ds(h, 1)]
                            if a == 1:
                                at = i * P
                                nc.vector.tensor_tensor(masked[:, :], ps[:, qb, at:at + P], cmask[:, :], ALU.add)
                                flat = ps[:, :, :].rearrange("p b t -> p (b t)")
                                n = qb * BLK + at
                                if n:
                                    nc.vector.tensor_reduce(mpart[:, 0:1], flat[:, 0:n], AX.X, ALU.max)
                                else:
                                    nc.vector.memset(mpart[:, 0:1], -3e38)
                                nc.vector.engine_nop()
                                nc.vector.tensor_reduce(mpart[:, 1:2], masked[:, :], AX.X, ALU.max)
                                nc.vector.drain()
                                tt(to, mpart[:, 0:1], mpart[:, 1:2], ALU.max).then_inc(s["gen_f"][qb], 1)
                            else:
                                nc.vector.tensor_reduce(to, ps[:, 0:4, :], AX.XY, ALU.max).then_inc(s["gen_f"][qb], 1)
                    dve.wait_ge(s["gen_s"][qb], H * TB + 1)
                    ts(negc[:, qb * BLK:(qb + 1) * BLK], ps[0:H, 7, :], -1.0, None, ALU.mult)
                    nc.vector.drain()
                nc.vector.tensor_copy(negf[:, :], negc[:, qb * BLK:(qb + 1) * BLK]).then_inc(s["final"], 1)

            def evac(a, n, done):
                s = A[a]
                dve.wait_ge(s["pv"], RING + done)
                nc.vector.tensor_copy(accs[:, :], acc).then_inc(s["evac"], 1)

            def norm(a, n, g):
                s = A[a]
                dve.wait_ge(s["pt"], n + 1)
                v = psT.rearrange("p (i h c) -> p i h c", i=TB, h=HG)
                nc.vector.reciprocal(rec[:, :, :], v[:, :, :, DK]).then_inc(s["recip"], 1)
                dve.wait_ge(s["recip"], n + 1)
                o = att[:, :, bass.ds(g * HG * DK, HG * DK)].rearrange("p i (h d) -> p i h d", h=HG)
                tt(o, v[:, :, :, 0:DK], rec[:, :, :].unsqueeze(3).to_broadcast([P, TB, HG, DK]), ALU.mult
                   ).then_inc(s["norm"], 1)

            def post(a, qb):
                s = A[a]
                dve.wait_ge(s["post_t"], qb + 1)
                nc.vector.tensor_copy(attT[:, :], ps[:, 6, :]).then_inc(s["post_e"], 1)
                dve.wait_ge(s["post_p"], qb + 1)
                xb = xn[:, qb * TB:(qb + 1) * TB, :]
                if a == 1:
                    dve.wait_ge(ld_x, 16)
                    dve.wait_ge(ld_w, 16 * 13)
                    tt(xb, xb, ps[:, 7, :].rearrange("p (i d) -> p i d", i=TB), ALU.add).then_inc(s["post_x"], 1)
                    dve.wait_ge(s["post_x"], qb + 1)
                    link(layernorm(xb, xb))
                else:
                    tt(ys[:, qb * TB:(qb + 1) * TB, :], xb, ps[:, 7, :].rearrange("p (i d) -> p i d", i=TB),
                       ALU.add).then_inc(s["post_x"], 1)
                    dve.wait_ge(s["post_x"], qb + 1)

            def attention(a):
                causal = a == 1
                general(a, 0)
                for qb in range(NB):
                    base, T = first_step(causal, qb), steps_of(causal, qb)
                    if qb:
                        norm(a, G * qb - 1, G - 1)
                        post(a, qb - 1)
                    if qb + 1 < NB:
                        general(a, qb + 1)
                    evac(a, G * qb, base + T)
                    with dve.Fori(1, G) as g:
                        norm(a, G * qb + g - 1, g - 1)
                        evac(a, G * qb + g, base + (g + 1) * T)
                norm(a, G * NB - 1, G - 1)
                post(a, NB - 1)

            ys = xT[:, :].rearrange("p (t d) -> p t d", t=S // P)
            nc.vector.memset(kaf[64:96, :], 0.0)
            nc.vector.memset(kaf[96:97, :], float(np.uint32(0x3F803F80).view(np.float32))).then_inc(init, 1)
            dve.wait_ge(ld_w, 16 * 13)
            nc.vector.tensor_copy(blk[:, :], blkf[:, :])
            nc.vector.memset(ones16[:, :], 1.0).then_inc(init, 1)
            dve.wait_ge(init, 3)
            for b in range(NB):
                split_q(1, b)
                take_norms(1, b)
                shift(1, b)
            attention(1)
            for b in range(NB):
                s = A[2]
                if b:
                    dve.wait_ge(s["zT"], 2 * b)
                layernorm(zb, xn[:, b * TB:(b + 1) * TB, :]).then_inc(s["zT"], 1)
                dve.wait_ge(s["zT"], 2 * b + 2)
                if b:
                    dve.wait_ge(s["v_proj"], b)
                else:
                    dve.wait_ge(A[1]["pv"], RING + first_step(True, NB))
                ts(hT, psT, ln[:, 0:1], ln[:, 1:2], ALU.mult, ALU.add).then_inc(s["hT"], 1)
                split_q(2, b)
                take_norms(2, b)
            for b in range(NB):
                lows(b)
                shift(2, b)
            attention(2)
            dve.wait_ge(ld_e, 16)
            link(nc.vector.tensor_copy(esel, eself))
            for b in range(NB):
                xb, y = xn[:, b * TB:(b + 1) * TB, :], ys[:, b * TB:(b + 1) * TB, :]
                layernorm(zb, y).then_inc(m_z, 1)
                dve.wait_ge(m_zT, b + 1)
                ts(hT, psT, ln[:, 2:3], ln[:, 3:4], ALU.mult, ALU.add).then_inc(m_h, 1)
                link(tt(xb, xb, y, ALU.add))
                dve.wait_ge(m_g, b + 1)
                link(tt(lg, ps[:, 6, 0:TB * E].rearrange("p (i e) -> p i e", i=TB),
                        gb[:, :].unsqueeze(1).to_broadcast([P, TB, E]), ALU.add))
                for i in range(TB):
                    link(nc.vector.max(mx8[:, i, :], lg[:, i, :]))
                    link(nc.vector.max_index(ix8[:, i, :], mx8[:, i, :], lg[:, i, :]))
                link(nc.vector.tensor_copy(ixf, ix8[:, :, 0]))
                for i in range(TB):
                    ins = ts(oh[:, i, :], iota[:, :], ixf[:, i:i + 1], None, ALU.is_equal)
                ins.then_inc(m_oh, 1)
                dve.wait_ge(m_ohT, b + 1)
                nc.vector.tensor_copy(ohT, ps[0:E, 7, :]).then_inc(m_ohTs, 1)
                for c in range(TB):
                    dve.wait_ge(m_hid, b * TB + c + 1)
                    for e in range(E):
                        n = b * TB * E + c * E + e
                        if n >= TB:
                            dve.wait_ge(m_hd, n - TB + 1)
                        tt(he[:, n % TB, :], hid[:, c, :], ms[:, e, :], ALU.mult).then_inc(m_he, 1)
                dve.wait_ge(m_hd, (b + 1) * TB * E)
                nc.vector.tensor_copy(yT, ps[:, 4, :]).then_inc(m_yT, 1)
                dve.wait_ge(m_yn, b + 1)
                link(tt(xb, xb, ps[:, 7, :].rearrange("p (i d) -> p i d", i=TB), ALU.add))
                if b:
                    dve.wait_ge(m_done, 16 * b)
                layernorm(ob, xb).then_inc(m_out, 1)


def kernel(**inputs):
    import concourse.bacc as _bacc
    from concourse.bass_utils import run_bass_kernel_spmd as _run

    def by_column(w, swapped=False):
        w = np.asarray(w).reshape(D, H, DK // 2, 2)
        return (w[:, :, :, ::-1] if swapped else w).reshape(D, H, DK).transpose(0, 2, 1).reshape(D, D)

    x = inputs["L0_attn_x"].reshape(S, D)
    wq = np.asarray(inputs["L0_attn_q_proj_weight"]).T
    wk = np.asarray(inputs["L0_attn_k_proj_weight"]).T
    wv = np.asarray(inputs["L0_attn_v_proj_weight"]).T
    wqkv = np.asarray(inputs["L0_ffn_w_qkv"])
    inv = (1.0 / THETA ** (np.arange(0, DK, 2, dtype=np.float32) / np.float32(DK))).astype(np.float32)
    ang = np.arange(S, dtype=np.float32)[None, :] * inv[:, None]
    c, s = np.cos(ang).astype(np.float32), np.sin(ang).astype(np.float32)
    cos = np.repeat(np.repeat(c, 2, axis=0), H, axis=0)
    sin = np.repeat(np.stack([-s, s], axis=1).reshape(DK, S), H, axis=0)
    p = np.arange(P)
    given = dict(
        xT=np.asarray(x).T, x=x, wa=np.concatenate([by_column(wq), by_column(wq, True), by_column(wk), by_column(wk, True), wv], axis=1),
        wo=np.asarray(inputs["L0_attn_o_proj_weight"]).T, wqkv=np.concatenate([by_column(wqkv[:, 0:D]), by_column(wqkv[:, D:2 * D]), wqkv[:, 2 * D:]], axis=1), wproj=inputs["L0_ffn_w_proj"],
        ln1w=inputs["L0_ffn_ln1_w"].reshape(D, 1), ln1b=inputs["L0_ffn_ln1_b"].reshape(D, 1),
        ln2w=inputs["L0_ffn_ln2_w"].reshape(D, 1), ln2b=inputs["L0_ffn_ln2_b"].reshape(D, 1),
        gw=inputs["L0_ffn_gate_w"], gb=np.tile(np.asarray(inputs["L0_ffn_gate_b"]).reshape(1, E), (P, 1)),
        w1=inputs["L0_ffn_w1"], w2=inputs["L0_ffn_w2"],
        cos=cos, sin=sin, ident=np.eye(P, dtype=np.float32),
        blk=(p[:, None] % H == np.arange(H)[None, :]).astype(np.float32),
        esel=(np.arange(E * P)[None, :] // P == np.arange(E)[:, None]).astype(np.float32),
        cmask=np.where(p[None, :] > p[:, None], -3e38, 0.0).astype(np.float32),
        iota=np.tile(np.arange(E, dtype=np.float32), (P, 1)),
    )
    nc = _bacc.Bacc("TRN2", target_bir_lowering=False, num_devices=1)
    arrays, args = {}, []
    for name, a in given.items():
        a = np.ascontiguousarray(a)
        arrays[f"in_{name}"] = a
        args.append(nc.dram_tensor(f"in_{name}", a.shape, mybir.dt.from_np(a.dtype), kind="ExternalInput").ap())
    out = nc.dram_tensor("out_0", (S, D), F32, kind="ExternalOutput").ap()
    build(nc, *args, out)
    r = _run(nc, [arrays], core_ids=[0])
    return r.results[0]["out_0"].reshape(1, S, D)
```

```python
from contextlib import ExitStack

import numpy as np

import concourse.bass as bass
from concourse import mybir

ALU = mybir.AluOpType
ACT = mybir.ActivationFunctionType
AX = mybir.AxisListType
F32 = mybir.dt.float32
BF16 = mybir.dt.bfloat16
U32 = mybir.dt.uint32
I32 = mybir.dt.int32

S = 2048
D = 128
H = 16
DK = D // H
E = 8
HID = 4 * D
EPS = 1e-5
THETA = 10000.0
P = 128

NP = 3
ROWS = NP * NP * DK
SHIFT_ROW = 96
KR = SHIFT_ROW + 1
BLK = 512
NB = S // BLK
TB = BLK // P
G = 4
HG = H // G
SCALE = float(1.0 / np.sqrt(DK))
VW = DK + 1
NSUB = 64
RING = 4

UNDER = 64.0 / SCALE
SPAN = 124.0 / SCALE


WSLOTS = 3
PSLOTS = 4
SIDE_FIRST, SIDE_LAST = 18, 30
UNROLLED = 2


def steps_of(causal, qb):
    return TB * (qb + 1) if causal else S // P


def first_step(causal, qb):
    return sum(G * steps_of(causal, b) for b in range(qb))


def ring_steps(causal, qb):
    return sum(1 + (G - UNROLLED) * steps_of(causal, b) for b in range(qb))


def pre_step(c):
    n, steps = 2 * TB * E, SIDE_LAST + 1 - SIDE_FIRST
    return next(k for k in range(steps) if n * (k + 1) // steps >= (c + 1) * E) + SIDE_FIRST - S // P


def build(nc, xT_d, x_d, wa_d, wo_d, wqkv_d, wproj_d, ln1w_d, ln1b_d, ln2w_d, ln2b_d, gw_d, gb_d,
          w1_d, w2_d, cos_d, sin_d, ident_d, blk_d, cmask_d, iota_d, out_d):
    ctx = ExitStack()
    with ctx:
        def sb(name, shape, dt=F32):
            return ctx.enter_context(nc.sbuf_tensor(name, shape, dt))

        def sem(name):
            return ctx.enter_context(nc.semaphore(name))

        KA = sb("key_rows", [P, H * S], BF16)
        QA = sb("query_rows", [P, 2 * H * BLK], BF16)
        parts = sb("parts", [P, 4 * NP * BLK], BF16)
        q3 = parts[:, 0:2 * NP * BLK].rearrange("p (s j t) -> p s j t", s=2, j=NP)
        k3 = parts[:, 2 * NP * BLK:].rearrange("p (s j t) -> p s j t", s=2, j=NP)
        wring = parts[:, :].bitcast(F32).rearrange("p (s e n) -> p s e n", s=WSLOTS, e=E)
        V = sb("values", [P, (S // P) * H * VW])
        vring = sb("values_ring", [P, RING, HG, VW])
        Pr = sb("probs", [P, 2, HG, BLK])
        xn = sb("x_rows", [P, S // P, D])
        early = sb("early_late", [P, 3 * S])
        xT, cos, sin = (early[:, n * S:(n + 1) * S] for n in range(3))
        v2 = early[:, 0:S].rearrange("p (k h d) -> p k h d", k=S // P, h=H)
        hid = early[:, 0:S].rearrange("p (c t) -> p c t", c=TB)
        prod = early[:, S:2 * S].rearrange("p (c t) -> p c t", c=PSLOTS)
        ms = early[:, 2 * S:3 * S].bitcast(BF16).rearrange("p (e t) -> p e t", e=E)
        wa = sb("w_attn1", [P, 5 * D])
        wo = sb("w_out1", [P, D])
        wqkv = sb("w_attn2", [P, 3 * D])
        wproj = sb("w_out2", [P, D])
        qa = sb("q_work", [P, BLK])
        qr = sb("q_rotated", [P, BLK])
        ka = sb("k_work", [P, BLK])
        kr = sb("k_rotated", [P, BLK])
        accs, attT = qr, kr
        yT = qa
        sqk = sb("squares_blockdiag", [P, 3 * BLK + H * NSUB], BF16)
        sq = sqk[:, 0:3 * BLK].rearrange("p (n t) -> p n t", n=3)
        kblk = sqk[:, 3 * BLK:]
        tg = sqk[:, 0:4 * BLK].bitcast(F32).rearrange("p (n t) -> p n t", n=2)
        zb = sb("z_rows", [P, TB, D])
        att = sb("attn_rows", [P, TB, D])
        hT = sb("h_cols", [P, BLK])
        yb = wa[:, 0:TB * D].rearrange("p (i d) -> p i d", i=TB)
        ident = sb("ident", [P, P])
        blkf = sb("blk_f", [P, H])
        blk = sb("blk", [P, H], BF16)
        cmask = sb("cmask", [P, P])
        masked = sb("masked", [P, P])
        ln = sb("ln_wb", [P, 4])
        gw = sb("gate_w", [P, E])
        gb = sb("gate_b", [P, E])
        iota = sb("iota", [P, E])
        rec = sb("recip", [P, TB, HG])
        mnat = sb("row_max", [P, TB, H])
        mpart = sb("row_max_parts", [P, 2])
        nq = sb("q_norms", [P, S // P, H])
        low = sb("row_low", [P, S // P, H])
        bound = sb("row_bound", [P, S // P, H])
        shf = sb("row_shift", [P, S // P, H])
        sw1 = sb("shift_work", [P, 3, TB, H])
        sw2 = Pr[:, :, :, :].rearrange("p s h t -> p (s h t)")[:, 0:3 * S // P * H].rearrange(
            "p (n k h) -> p n k h", n=3, k=S // P)
        kmx = sb("k_norm_max", [H, 2])
        kdg = sb("k_norm_diag", [H, H])
        kmb = sb("k_norm_rows", [P, H])
        oks = sb("row_ok", [P, 2])
        negc = sb("neg_shift", [H, S], BF16)
        negf = sb("neg_shift_final", [H, BLK], BF16)
        onesf = sb("ones_f", [P, P])
        flags = sb("flags", [1, 2 * NB], I32)
        st = sb("ln_stats", [P, TB, 6])
        mv = sb("ln_meanvar", [P, TB, 2])
        nw = sb("ln_newton", [P, 4, TB])
        lg = sb("logits", [P, TB, E])
        mx8 = sb("logit_max", [P, TB, 8])
        ix8 = sb("logit_at", [P, TB, 8], U32)
        ixf = sb("logit_at_f", [P, TB])
        oh = sb("onehot", [P, TB, E])
        ohT = sb("onehot_T", [E, BLK], BF16)
        esel = sb("expert_rows", [E, E * P], BF16)
        k_scratch = nc.dram_tensor("k_scratch", (2, NP, DK, H, S), BF16, kind="Internal").ap()
        q_scratch = nc.dram_tensor("q_scratch", (2, NP, DK, H, S), BF16, kind="Internal").ap()

        ps = ctx.enter_context(nc.psum_tensor("ps", [P, 8, BLK], F32))
        acc, psT = ps[:, 4, :], ps[:, 5, :]
        psT4 = psT.rearrange("p (i d) -> p i d", i=TB)
        ps6, ps7 = ps[:, 6, :], ps[:, 7, :]
        ps7r = ps7.rearrange("p (i d) -> p i d", i=TB)

        ld_a, ld_w, ld_x, ld_e = (sem(n) for n in ("ld_a", "ld_w", "ld_x", "ld_e"))
        ld_b = [sem(f"ld_b{b}") for b in range(NB)]
        ld_m = [sem(f"ld_m{n}") for n in range(WSLOTS)]
        init, scratch_out = sem("init"), sem("scratch_out")
        dch, pch = sem("dve_chain"), sem("pool_chain")
        A = {}
        for a in (1, 2):
            s = {}
            for n in ("q_proj", "k_proj", "v_proj", "q_taken", "k_taken", "v_taken", "q_split", "k_split",
                      "sq_q", "sq_k", "nk_mm", "nk_max", "kdiag", "kmb_mm", "nq_mm", "nq_taken",
                      "shift", "shiftT", "negc", "ok", "ok_mm", "flag", "final",
                      "S", "exp", "pv", "v", "evac", "recip", "pt", "norm", "post_t", "post_e", "post_p",
                      "post_x"):
                s[n] = sem(f"a{a}_{n}")
            for n in ("gen_s", "gen_f", "gen_d"):
                s[n] = [sem(f"a{a}_{n}{b}") for b in range(NB)]
            for n in ("k_rows", "q_rows"):
                s[n] = [sem(f"a{a}_{n}{b}") for b in range(2)]
            s["c_row"] = sem(f"a{a}_c_row")
            A[a] = s
        dg_seen = sem("dg_seen")
        A[1]["dg"] = sem("a1_cut")
        k_early = sem("k_rows_early")
        z, zT, hTs, kbd, low_mm, low_taken, v_moved = (
            sem(n) for n in ("a2_z", "a2_zT", "a2_hT", "k_blockdiag_set", "low_mm", "low_taken", "v_moved"))
        m_z, m_zT, m_h, m_g, m_oh, m_ohT, m_ohTs = (sem(f"m_{n}") for n in ("z", "zT", "h", "g", "oh", "ohT", "ohTs"))
        m_mk, m_ms, m_pd, m_pp, m_mm, m_xh, m_arg, m_tanh, m_hid, m_yT, m_yn, m_out, m_done = (
            sem(f"m_{n}") for n in ("mask_mm", "mask", "prod_dve", "prod_pool", "mm", "pre_copied",
                                    "tanh_arg", "tanh", "hid", "yT", "yn", "out", "done"))

        KAv = KA[:, :].rearrange("p (h t) -> p h t", h=H)
        QAv = QA[:, :].rearrange("p (s h t) -> p s h t", s=2, h=H)
        Vv = V[:, :].rearrange("p (k h w) -> p k h w", h=H, w=VW)
        kaf, qaf = KA[:, :].bitcast(F32), QA[:, :].bitcast(F32)

        block = ctx.enter_context(nc.Block())

        @block.sync
        def _(sp):
            sp.dma_start(wa[:, :], wa_d).then_inc(ld_a, 16)
            for b in range(NB):
                c = slice(b * BLK, (b + 1) * BLK)
                sp.dma_start(xT[:, c], xT_d[:, c]).then_inc(ld_b[b], 16)
                sp.dma_start(cos[:, c], cos_d[:, c]).then_inc(ld_b[b], 16)
                sp.dma_start(sin[:, c], sin_d[:, c]).then_inc(ld_b[b], 16)
                if b == 0:
                    for t, s in ((blkf, blk_d), (ident, ident_d)):
                        sp.dma_start(t[:, :], s).then_inc(ld_w, 16)
            for t, s in ((cmask, cmask_d), (wo, wo_d), (wqkv, wqkv_d), (wproj, wproj_d), (gw, gw_d),
                         (iota, iota_d), (gb, gb_d)):
                sp.dma_start(t[:, :], s).then_inc(ld_e, 16)
            for n, s in enumerate((ln1w_d, ln1b_d, ln2w_d, ln2b_d)):
                sp.dma_start(ln[:, n:n + 1], s).then_inc(ld_e, 16)
            sp.dma_start(xn[:, :, :], x_d.rearrange("(t p) d -> p t d", p=P)).then_inc(ld_x, 16)

            parts_out = [0]

            def to_scratch(p3, scratch, b):
                sp.dma_start(scratch[:, :, :, b * BLK:(b + 1) * BLK].rearrange("j d h t -> (d h) j t"), p3
                             ).then_inc(scratch_out, 16)
                parts_out[0] += 16

            def scratch_written():
                sp.wait_ge(scratch_out, parts_out[0])

            def key_rows(a, heads, t0, t1, done):
                src = k_scratch[a - 1].rearrange("j d h t -> (j d) h t")
                for i in range(NP):
                    for j in range(NP):
                        r = (i * NP + j) * DK
                        sp.dma_start(KAv[r:r + DK, heads, t0:t1], src[i * DK:(i + 1) * DK, heads, t0:t1]
                                     ).then_inc(done, 16)

            def query_rows(a, b):
                src = q_scratch[a - 1, :, :, :, b * BLK:(b + 1) * BLK].rearrange("j d h t -> (j d) h t")
                for i in range(NP):
                    r = i * NP * DK
                    sp.dma_start(QAv[r:r + NP * DK, b % 2, :, :], src).then_inc(A[a]["q_rows"][b % 2], 16)

            def shift_row(a, b):
                sp.wait_ge(A[a]["final"], b + 1)
                sp.dma_start(QAv[SHIFT_ROW:SHIFT_ROW + 1, b % 2, :, :], negf[:, :]).then_inc(A[a]["c_row"], 16)

            def slot_free(a, b):
                if b >= 2:
                    sp.wait_ge(A[a]["S"], 2 * first_step(a == 1, b - 1))
                elif a == 2:
                    sp.wait_ge(A[1]["S"], 2 * first_step(True, NB - 1 + b))

            sp.wait_ge(init, 3)
            for b in range(NB):
                sp.wait_ge(A[1]["q_split"], b + 1)
                to_scratch(q3[:, b % 2], q_scratch[0], b)
                sp.wait_ge(A[1]["k_split"], b + 1)
                to_scratch(k3[:, b % 2], k_scratch[0], b)
                scratch_written()
                key_rows(1, slice(0, H), b * BLK, (b + 1) * BLK, A[1]["k_rows"][b % 2])
                if b < 2:
                    query_rows(1, b)
            shift_row(1, 0)
            for qb in range(1, NB):
                if qb >= 2:
                    slot_free(1, qb)
                    query_rows(1, qb)
                shift_row(1, qb)
                sp.wait_ge(A[2]["q_split"], qb)
                to_scratch(q3[:, (qb - 1) % 2], q_scratch[1], qb - 1)
                sp.wait_ge(A[2]["k_split"], qb)
                to_scratch(k3[:, (qb - 1) % 2], k_scratch[1], qb - 1)
            scratch_written()
            slot_free(2, 0)
            query_rows(2, 0)
            last = NB - 1
            for g in range(G):
                sp.wait_ge(A[1]["S"], 2 * (first_step(True, last) + (g + 1) * steps_of(True, last)))
                key_rows(2, slice(g * HG, (g + 1) * HG), 0, last * BLK, k_early)
            sp.wait_ge(A[2]["q_split"], NB)
            to_scratch(q3[:, last % 2], q_scratch[1], last)
            sp.wait_ge(A[2]["k_split"], NB)
            to_scratch(k3[:, last % 2], k_scratch[1], last)
            scratch_written()
            key_rows(2, slice(0, H), last * BLK, S, A[2]["k_rows"][0])
            query_rows(2, 1)
            shift_row(2, 0)

            def expert_weights(n):
                b, c = n // (2 * TB), n % (2 * TB)
                if n >= WSLOTS:
                    sp.wait_ge(m_mm, (n - WSLOTS + 1) * E)
                u = slice(c % TB * P, (c % TB + 1) * P)
                src = w1_d[:, :, u] if c < TB else w2_d[:, u, :]
                sp.dma_start(wring[:, n % WSLOTS], src.rearrange("e p n -> p e n")).then_inc(ld_m[n % WSLOTS], 16)

            def rows_out(b):
                sp.wait_ge(m_out, b + 1)
                sp.dma_start(out_d[b * BLK:(b + 1) * BLK, :].rearrange("(i p) d -> p i d", p=P), zb[:, :, :]
                             ).then_inc(m_done, 16)

            sp.wait_ge(low_mm, S // P)
            for n in range(WSLOTS):
                expert_weights(n)
            for qb in range(1, NB + 1):
                if qb < NB:
                    if qb >= 2:
                        slot_free(2, qb)
                        query_rows(2, qb)
                    shift_row(2, qb)
                for n in range(2 * TB):
                    n += (qb - 1) * 2 * TB + WSLOTS
                    if n < NB * 2 * TB:
                        expert_weights(n)
                rows_out(qb - 1)
            sp.wait_ge(m_done, 16 * NB)

        @block.tensor
        def _(pe):
            def mm(out, l, r, start=True, stop=True):
                return nc.tensor.matmul(out, l, r, start=start, stop=stop, skip_group_check=True)

            def turned(out, rows, m=P):
                for i in range(TB):
                    last = nc.tensor.transpose(out[0:m, i * P:(i + 1) * P], rows(i), ident[:, :])
                return last

            def project1(b):
                s = A[1]
                pe.wait_ge(ld_b[b], 48)
                src = xT[:, b * BLK:(b + 1) * BLK]
                for n in range(4):
                    name = "q" if n < 2 else "k"
                    pe.wait_ge(s[name + "_taken"], b)
                    mm(ps[:, n, :], wa[:, n * D:(n + 1) * D], src).then_inc(s[name + "_proj"], 1)
                pe.wait_ge(s["v_taken"], b)
                for i in range(TB):
                    last = mm(ps[:, 4, i * D:(i + 1) * D], src[:, i * P:(i + 1) * P], wa[:, 4 * D:5 * D])
                last.then_inc(s["v_proj"], 1)

            def project2(b):
                s = A[2]
                pe.wait_ge(hTs, b + 1)
                mm(ps6, wqkv[:, 0:D], hT[:, :]).then_inc(s["q_proj"], 1)
                mm(ps7, wqkv[:, D:2 * D], hT[:, :]).then_inc(s["k_proj"], 1)

            def project2_values(b):
                s = A[2]
                pe.wait_ge(s["q_taken"], b + 1)
                for i in range(TB):
                    last = mm(ps[:, 6, i * D:(i + 1) * D], hT[:, i * P:(i + 1) * P], wqkv[:, 2 * D:3 * D])
                last.then_inc(s["v_proj"], 1)

            def key_norms(a, b):
                s = A[a]
                if a == 1 and b == 0:
                    pe.wait_ge(init, 3)
                pe.wait_ge(s["sq_k"], b + 1)
                if a == 1:
                    pe.wait_ge(s["nk_max"], b)
                mm(ps[0:H, 7, :], blk[:, :], sq[:, 1, :]).then_inc(s["nk_mm"], 1)

            def key_bound(a, n, t):
                s = A[a]
                pe.wait_ge(s["kdiag"], n)
                mm(ps[:, 7, 0:H], onesf[0:H, :], kdg[:, :]).then_inc(s["kmb_mm"], 1)

            def query_norms(a, b):
                s = A[a]
                pe.wait_ge(s["sq_q"], b + 1)
                pe.wait_ge(s["v_taken" if a == 2 else "nq_taken"], b + (a == 2))
                for n in range(2 if a == 1 else 1):
                    for i in range(TB):
                        at = (n * TB + i) * H
                        last = mm(ps[:, 6, at:at + H], sq[:, 2 * n, i * P:(i + 1) * P], blk[:, :])
                last.then_inc(s["nq_mm"], 1)

            def lows(b, i):
                t = b * TB + i
                if t == 0:
                    pe.wait_ge(kbd, 1)
                pe.wait_ge(A[2]["nq_taken"], b + 1)
                pe.wait_ge(low_taken, t)
                for c in range(H * NSUB // BLK):
                    last = mm(ps[:, 6 + c, :], q3[:, b % 2, 0, i * P:(i + 1) * P], kblk[:, c * BLK:(c + 1) * BLK])
                last.then_inc(low_mm, 1)

            def shift_turn(a, b, n):
                s = A[a]
                pe.wait_ge(s["shift"], n)
                turned(ps7, lambda i: shf[:, b * TB + i, :], H).then_inc(s["shiftT"], 1)

            def count_ok(a, n):
                s = A[a]
                pe.wait_ge(s["ok"], n)
                mm(ps[0:1, 6, 0:1], oks[:, 1:2], onesf[:, 0:1]).then_inc(s["ok_mm"], 1)

            def general(a, qb, base):
                s = A[a]
                f = (a - 1) * NB + qb
                pe.wait_ge(s["flag"], qb + 1 if a == 1 else 1)
                bad = pe.value_load(flags[0:1, f:f + 1], min_val=0, max_val=P)
                with pe.If(bad != 0):
                    pe.wait_ge(s["q_rows"][qb % 2], 16 * NP * (qb // 2 + 1))
                    pe.wait_ge(s["exp"], 2 * base + 2)
                    with pe.Fori(0, H) as h:
                        for i in range(TB):
                            nk = qb * BLK + (i + 1) * P if a == 1 else S
                            pe.wait_ge(s["gen_f"][qb], h * TB + i + 1)
                            for c in range(0, nk, BLK):
                                n = min(BLK, nk - c)
                                last = mm(ps[:, c // BLK, 0:n],
                                          QA[0:ROWS, bass.ds(h * BLK + (qb % 2) * H * BLK + i * P, P)],
                                          KA[0:ROWS, bass.ds(h * S + c, n)])
                            last.then_inc(s["gen_s"][qb], 1)
                    pe.wait_ge(s["gen_f"][qb], H * TB + 1)
                    turned(ps7, lambda i: mnat[:, i, :], H).then_inc(s["gen_s"][qb], 1)

            def scores(s, slot, g, kt_at, t, lo):
                for p in range(2):
                    pe.wait_ge(s["exp"], 2 * t + p + 1)
                    for hh in range(2):
                        h = g * HG + 2 * p + hh
                        last = mm(ps[:, 2 * p + hh, lo:BLK], KA[0:KR, bass.ds(h * S + kt_at, P)],
                                  QA[0:KR, bass.ds(h * BLK + slot * H * BLK + lo, BLK - lo)])
                    last.then_inc(s["S"], 1)

            def values(a, step, n):
                s = A[a]
                t, i, lo = step["t"], step["i"], step["lo"]
                if step["ring"] is not None:
                    pe.wait_ge(s["v"], step["ring"])
                pe.wait_ge(s["exp"], 2 * t + 4)
                if step["cut"] is not None:
                    pe.wait_ge(s["dg"], step["cut"])
                if step["start"] and not (isinstance(n, int) and n == 0):
                    pe.wait_ge(s["evac"], n)
                for hh in range(HG):
                    w = vring[:, i, hh, :] if step["ring"] is not None else Vv[:, step["kt"], step["g"] * HG + hh, :]
                    last = mm(acc[32 * hh:32 * hh + VW, lo:BLK], w, Pr[:, i % 2, hh, lo:BLK],
                              start=step["start"], stop=step["stop"])
                last.then_inc(s["pv"], 1)

            def turn(a, n):
                s = A[a]
                pe.wait_ge(s["evac"], n + 1)
                turned(psT, lambda i: accs[:, i * P:(i + 1) * P]).then_inc(s["pt"], 1)

            def post_turn(a, qb):
                s = A[a]
                pe.wait_ge(s["norm"], G * (qb + 1))
                turned(ps6, lambda i: att[:, i, :]).then_inc(s["post_t"], 1)

            def post_project(a, qb):
                s = A[a]
                pe.wait_ge(s["post_e"], qb + 1)
                for i in range(TB):
                    last = mm(ps[:, 7, i * D:(i + 1) * D], attT[:, i * P:(i + 1) * P], (wo if a == 1 else wproj)[:, :])
                last.then_inc(s["post_p"], 1)

            def z_turn(b):
                pe.wait_ge(z, b + 1)
                turned(ps6, lambda i: zb[:, i, :]).then_inc(zT, 1)

            def m_turn(b):
                pe.wait_ge(m_z, b + 1)
                turned(ps6, lambda i: zb[:, i, :]).then_inc(m_zT, 1)

            def m_gate(b):
                pe.wait_ge(m_h, b + 1)
                for i in range(TB):
                    last = mm(ps[:, 7, i * E:(i + 1) * E], hT[:, i * P:(i + 1) * P], gw[:, :])
                last.then_inc(m_g, 1)

            def m_onehot(b):
                pe.wait_ge(m_oh, b + 1)
                turned(ps7, lambda i: oh[:, i, :], E).then_inc(m_ohT, 1)

            def m_masks(b, e0, e1):
                pe.wait_ge(m_ohTs, b + 1)
                for e in range(e0, e1):
                    pe.wait_ge(m_ms, b * E + max(0, e - 1))
                    mm(ps[:, 6 + e % 2, :], esel[:, e * P:(e + 1) * P], ohT[:, :]).then_inc(m_mk, 1)

            def m_products(b, k0, k1):
                for k in range(k0, k1):
                    n = b * 2 * TB * E + k
                    c, e = k // E, k % E
                    if e == 0:
                        ch = n // E
                        pe.wait_ge(ld_m[ch % WSLOTS], 16 * (ch // WSLOTS + 1))
                        if c == 0:
                            pe.wait_ge(m_ms, (b + 1) * E)
                        if 2 <= c < TB:
                            pe.wait_ge(m_xh, b * TB + c - 1)
                        if c == TB:
                            pe.wait_ge(m_xh, b * TB + TB - 1)
                    pe.wait_ge(m_pd if n % 2 == 0 else m_pp, n // 2 + 1)
                    if c < TB:
                        out, start, stop = ps[:, 6 + c % 2, :], e == 0, e == E - 1
                    else:
                        out, start, stop = ps6, k == TB * E, k == 2 * TB * E - 1
                    mm(out, wring[:, (n // E) % WSLOTS, e, :], prod[:, n % PSLOTS, :], start, stop).then_inc(m_mm, 1)

            def m_back(b):
                pe.wait_ge(m_yT, b + 1)
                turned(ps7, lambda i: yT[:, i * P:(i + 1) * P]).then_inc(m_yn, 1)

            def group(a, qb, g, n, pending, side):
                s = A[a]
                causal = a == 1
                T = steps_of(causal, qb)
                t0 = first_step(causal, qb) + g * T
                full = qb if causal else NB
                looped = not isinstance(g, int)
                ring0 = ring_steps(causal, qb) + 1 + (g - UNROLLED) * T if looped else None
                pos = [0]
                g_last = not looped and g == UNROLLED - 1

                def step(kb, i, diag, opening):
                    nonlocal pending
                    lo = i * P if diag else 0
                    at = kb * TB + i
                    scores(s, qb % 2, g, kb * BLK + i * P, t0 + at, lo)
                    if pending is not None:
                        values(a, pending, n)
                    pending = dict(t=t0 + at, i=i, lo=lo, g=g, kt=at, ring=ring0 + at + 1 if looped else None,
                                   cut=n * TB + i + 1 if diag else None, start=opening and i == 0, stop=False)
                    if opening and i == 2 and not (isinstance(n, int) and n == 0):
                        turn(a, n - 1)
                    for f in side.get(pos[0], ()):
                        f()
                    pos[0] += 1

                def steps(kb, diag, opening):
                    for i in range(TB):
                        step(kb, i, diag, opening)

                steps(0, full == 0, True)
                if full > 1:
                    if looped:
                        t_in, r_in = t0 + TB - 1, ring0 + TB
                        with pe.Fori(1, full) as kb:
                            pending = dict(pending, t=t_in + (kb - 1) * TB, ring=r_in + (kb - 1) * TB)
                            steps(kb, False, False)
                        pending = dict(pending, t=t0 + full * TB - 1, ring=ring0 + full * TB)
                    else:
                        for kb in range(1, full):
                            steps(kb, False, False)
                if causal and full > 0:
                    steps(full, True, False)
                return last_step(a, qb, g) if g_last else dict(pending, stop=True)

            def last_step(a, qb, g):
                causal = a == 1
                T = steps_of(causal, qb)
                return dict(t=first_step(causal, qb) + (g + 1) * T - 1, i=TB - 1, lo=(TB - 1) * P if causal else 0,
                            ring=ring_steps(causal, qb) + 1 + (g + 1 - UNROLLED) * T,
                            cut=(G * qb + g + 1) * TB if causal else None, start=False, stop=True)

            def attention(a, side):
                causal = a == 1
                s = A[a]
                general(a, 0, 0)
                pending = None
                for qb in range(NB):
                    base, T = first_step(causal, qb), steps_of(causal, qb)
                    if causal:
                        pe.wait_ge(s["k_rows"][qb % 2], 16 * NP * NP * (qb // 2 + 1))
                    elif qb == 0:
                        pe.wait_ge(k_early, 16 * NP * NP * G)
                        pe.wait_ge(s["k_rows"][0], 16 * NP * NP)
                        pe.wait_ge(v_moved, 1)
                    pe.wait_ge(s["q_rows"][qb % 2], 16 * NP * (qb // 2 + 1))
                    pe.wait_ge(s["c_row"], 16 * (qb + 1))
                    todo = side(qb)
                    for g in range(UNROLLED):
                        here = {p - g * T: f for p, f in todo.items() if g * T <= p < (g + 1) * T}
                        if g == 1 and qb + 1 < NB:
                            general(a, qb + 1, base + T)
                        pending = group(a, qb, g, G * qb + g, pending, here)
                    with pe.Fori(UNROLLED, G) as g:
                        group(a, qb, g, G * qb + g, last_step(a, qb, g - 1), {})
                    pending = last_step(a, qb, G - 1)
                values(a, pending, 0)
                turn(a, G * NB - 1)

            def side1(qb):
                if qb == 0:
                    return {}
                T, b = steps_of(True, qb), qb - 1
                return {4: [lambda: post_turn(1, b)], 6: [lambda: post_project(1, b)],
                        T + 3: [lambda: z_turn(b)], T + 4: [lambda: project2(b)],
                        T + 5: [lambda: project2_values(b)], T + 6: [lambda: key_norms(2, b), lambda: query_norms(2, b)],
                        T + 7: [lambda i=i: lows(b, i) for i in range(TB)]}

            def side2(qb):
                if qb == 0:
                    return {}
                b = qb - 1
                todo = {4: [lambda: post_turn(2, b)], 6: [lambda: post_project(2, b)], 9: [lambda: m_turn(b)],
                        10: [lambda: m_gate(b)], 12: [lambda: m_onehot(b)]}
                for e in range(0, E, 2):
                    todo[13 + e // 2] = [lambda e=e: m_masks(b, e, e + 2)]
                first, last, n = SIDE_FIRST, SIDE_LAST, 2 * TB * E
                cuts = [n * k // (last + 1 - first) for k in range(last + 2 - first)]
                for k in range(last + 1 - first):
                    todo.setdefault(first + k, []).append(lambda k=k: m_products(b, cuts[k], cuts[k + 1]))
                todo[31] = [lambda: m_back(b)]
                return todo

            pe.wait_ge(ld_a, 16)
            for b in range(NB):
                project1(b)
                key_norms(1, b)
                key_bound(1, b + 1, b + 1)
                query_norms(1, b)
                shift_turn(1, b, b + 1)
                count_ok(1, b + 1)
            attention(1, side1)
            b = NB - 1
            post_turn(1, b)
            post_project(1, b)
            z_turn(b)
            project2(b)
            project2_values(b)
            key_norms(2, b)
            query_norms(2, b)
            for i in range(TB):
                lows(b, i)
            key_bound(2, 1, 1)
            for b in range(NB):
                if b:
                    pe.wait_ge(A[2]["negc"], b)
                shift_turn(2, b, 1)
            count_ok(2, 1)
            attention(2, side2)
            b = NB - 1
            post_turn(2, b)
            post_project(2, b)
            m_turn(b)
            m_gate(b)
            m_onehot(b)
            m_masks(b, 0, E)
            m_products(b, 0, 2 * TB * E)
            m_back(b)

        @block.scalar
        def _(act):
            def exps(a, t, i, lo):
                s = A[a]
                act.wait_ge(s["pv"], t + 3)
                for p in range(2):
                    act.wait_ge(s["S"], 2 * t + p + 1)
                    nc.scalar.activation(Pr[:, i % 2, 2 * p:2 * p + 2, lo:BLK], ps[:, 2 * p:2 * p + 2, lo:BLK],
                                         ACT.Exp, scale=SCALE).then_inc(s["exp"], 1)

            def group(a, qb, g, side):
                causal = a == 1
                full = qb if causal else NB
                t0 = first_step(causal, qb) + g * steps_of(causal, qb)

                def steps(kb, diag):
                    for i in range(TB):
                        exps(a, t0 + kb * TB + i, i, i * P if diag else 0)
                        if isinstance(kb, int):
                            for f in side.get(kb * TB + i, ()):
                                f()

                if full and isinstance(g, int) and side:
                    for kb in range(full):
                        steps(kb, False)
                elif full:
                    with act.Fori(0, full) as kb:
                        steps(kb, False)
                if causal:
                    steps(full, True)

            def pre_copy(b, c):
                act.wait_ge(m_mm, b * 2 * TB * E + (c + 1) * E)
                if c == 0 and b:
                    pass
                nc.scalar.activation(hid[:, c, :], ps[:, 6 + c % 2, :], ACT.Copy).then_inc(m_xh, 1)

            def tanh(b, c):
                act.wait_ge(m_arg, b * TB + c + 1)
                nc.scalar.activation(tg[:, c % 2, :], tg[:, c % 2, :], ACT.Tanh,
                                     scale=float(np.sqrt(2.0 / np.pi))).then_inc(m_tanh, 1)

            act.wait_ge(init, 3)
            for b in range(NB):
                act.wait_ge(A[1]["v_proj"], b + 1)
                nc.scalar.activation(Vv[:, b * TB:(b + 1) * TB, :, 0:DK],
                                     ps[:, 4, :].rearrange("p (i h d) -> p i h d", i=TB, h=H),
                                     ACT.Copy).then_inc(A[1]["v_taken"], 1)
            for qb in range(NB):
                with act.Fori(0, G) as g:
                    group(1, qb, g, {})
            for qb in range(NB):
                if qb == 0:
                    with act.Fori(0, G) as g:
                        group(2, qb, g, {})
                else:
                    b = qb - 1
                    group(2, qb, 0, {})
                    side = {}
                    for c in range(TB):
                        side.setdefault(pre_step(c), []).append(lambda c=c: pre_copy(b, c))
                        side.setdefault(pre_step(c) + 1, []).append(lambda c=c: tanh(b, c))
                    group(2, qb, 1, side)
                    with act.Fori(2, G) as g:
                        group(2, qb, g, {})
            b = NB - 1
            for c in range(TB):
                pre_copy(b, c)
                if c:
                    tanh(b, c - 1)
            tanh(b, TB - 1)

        @block.gpsimd
        def _(pool):
            chain = [0]

            def link(ins):
                chain[0] += 1
                ins.then_inc(pch, 1)
                pool.wait_ge(pch, chain[0])

            def split_k(b):
                s = A[1]
                pool.wait_ge(s["k_taken"], b + 1)
                if b >= 2:
                    pool.wait_ge(s["k_rows"][b % 2], 16 * NP * NP * (b // 2))
                link(nc.gpsimd.tensor_tensor(ka[:, :], ka[:, :], kr[:, :], ALU.add))
                kk = k3[:, b % 2]
                link(nc.gpsimd.tensor_copy(kk[:, 0, :], ka[:, :]))
                if b:
                    pool.wait_ge(s["nk_mm"], b)
                nc.gpsimd.tensor_tensor(sq[:, 1, :], ka[:, :], ka[:, :], ALU.mult).then_inc(s["sq_k"], 1)
                pool.wait_ge(s["sq_k"], b + 1)
                link(nc.gpsimd.tensor_tensor(ka[:, :], ka[:, :], kk[:, 0, :], ALU.subtract))
                link(nc.gpsimd.tensor_copy(kk[:, 1, :], ka[:, :]))
                nc.gpsimd.tensor_tensor(kk[:, 2, :], ka[:, :], kk[:, 1, :], ALU.subtract).then_inc(s["k_split"], 1)

            def cut(t, i):
                s = A[1]
                pool.wait_ge(s["exp"], 2 * t + 4)
                pool.sem_inc(dg_seen, 1)
                at = Pr[:, i % 2, :, i * P:(i + 1) * P]
                nc.gpsimd.affine_select(out=at, in_=at, compare_op=ALU.is_ge, fill=0.0, base=0,
                                        pattern=[[0, HG], [1, P]], channel_multiplier=-1).then_inc(s["dg"], 1)

            def group(a, qb, g, ring):
                s = A[a]
                causal = a == 1
                full = qb if causal else NB
                t0 = first_step(causal, qb) + g * steps_of(causal, qb)

                def copy_in(kb, i):
                    t = t0 + kb * TB + i
                    pool.wait_ge(s["pv"], t + 1)
                    nc.gpsimd.tensor_copy(
                        vring[:, i, :, :],
                        V[:, bass.ds((kb * TB + i) * H * VW + g * HG * VW, HG * VW)].rearrange(
                            "p (h w) -> p h w", h=HG)).then_inc(s["v"], 1)

                def steps(kb, diag):
                    for i in range(TB):
                        if ring:
                            copy_in(kb, i)
                        if diag:
                            cut(t0 + kb * TB + i, i)

                if full and ring:
                    with pool.Fori(0, full) as kb:
                        steps(kb, False)
                if causal:
                    steps(full, True)
                if not ring and g == UNROLLED - 1:
                    copy_in(steps_of(causal, qb) // TB - 1, TB - 1)

            def products(b, k0, k1):
                for k in range(k0, k1):
                    n = b * 2 * TB * E + k
                    if n % 2 == 0:
                        continue
                    c, e = k // E, k % E
                    if k == 1:
                        pool.wait_ge(m_ms, (b + 1) * E)
                    if n >= PSLOTS:
                        pool.wait_ge(m_mm, n - PSLOTS + 1)
                    if c >= TB:
                        pool.wait_ge(m_hid, b * TB + c - TB + 1)
                    nc.gpsimd.tensor_tensor(prod[:, n % PSLOTS, :], hT[:, :] if c < TB else hid[:, c - TB, :],
                                            ms[:, e, :], ALU.mult).then_inc(m_pp, 1)

            link(nc.gpsimd.memset(qaf[64:P, :], 0.0))
            link(nc.gpsimd.memset(V[:, :], 1.0))
            nc.gpsimd.memset(oks[:, :], 0.0).then_inc(init, 1)
            for a in (1, 2):
                pool.sem_inc(A[a]["pv"], RING)
                pool.sem_inc(A[a]["exp"], 2)
            for b in range(NB):
                split_k(b)
            for b in range(NB):
                pool.wait_ge(A[1]["v_taken"], b + 1)
            for a in (1, 2):
                causal = a == 1
                if a == 2:
                    pool.wait_ge(A[1]["pv"], RING + first_step(True, NB))
                    pool.wait_ge(A[2]["v_taken"], NB)
                    nc.gpsimd.tensor_copy(Vv[:, :, :, 0:DK], v2).then_inc(v_moved, 1)
                    pool.wait_ge(v_moved, 1)
                for qb in range(NB):
                    if not causal and qb:
                        products(qb - 1, 0, 2 * TB * E)
                    for g in range(UNROLLED):
                        group(a, qb, g, False)
                    with pool.Fori(UNROLLED, G) as g:
                        group(a, qb, g, True)
            products(NB - 1, 0, 2 * TB * E)

        @block.vector
        def _(dve):
            chain = [0]

            def link(ins):
                chain[0] += 1
                ins.then_inc(dch, 1)
                dve.wait_ge(dch, chain[0])

            tt, ts, copy = nc.vector.tensor_tensor, nc.vector.tensor_scalar, nc.vector.tensor_copy

            def mark(ins, s, n):
                ins.then_inc(s, 1)
                dve.wait_ge(s, n)

            def rsqrt(y, v, h, t, turns):
                link(ts(y.bitcast(I32), v.bitcast(I32), -0.5, 1597463007.0, ALU.mult, ALU.add))
                link(ts(h, v, -0.5, None, ALU.mult))
                for _ in range(turns):
                    link(tt(t, y, y, ALU.mult))
                    link(tt(t, t, h, ALU.mult))
                    link(nc.vector.scalar_tensor_tensor(out=y, in0=t, scalar=1.5, in1=y, op0=ALU.add, op1=ALU.mult))

            def layernorm(dst, src):
                for i in range(TB):
                    ins = nc.vector.bn_stats(st[:, i, :], src[:, i, :])
                link(ins)
                for i in range(TB):
                    ins = nc.vector.bn_aggr(mv[:, i, :], st[:, i, :])
                link(ins)
                v, y, h, t = (nw[:, n, :] for n in range(4))
                link(ts(v, mv[:, :, 1], EPS, None, ALU.add))
                rsqrt(y, v, h, t, 3)
                for i in range(TB):
                    ins = ts(dst[:, i, :], src[:, i, :], mv[:, i, 0:1], nw[:, 1, i:i + 1], ALU.subtract, ALU.mult)
                return ins

            def cut_in_parts(work, p3, square):
                link(copy(p3[:, 0, :], work))
                link(tt(square, work, work, ALU.mult))
                link(tt(work, work, p3[:, 0, :], ALU.subtract))
                link(copy(p3[:, 1, :], work))
                return tt(p3[:, 2, :], work, p3[:, 1, :], ALU.subtract)

            def split1(b):
                s = A[1]
                c = slice(b * BLK, (b + 1) * BLK)
                dve.wait_ge(ld_b[b], 48)
                dve.wait_ge(s["k_proj"], 2 * b + 2)
                dve.wait_ge(s["k_split"], b)
                tt(ka[:, :], ps[:, 2, :], cos[:, c], ALU.mult)
                tt(kr[:, :], ps[:, 3, :], sin[:, c], ALU.mult).then_inc(s["k_taken"], 1)
                dve.wait_ge(s["q_proj"], 2 * b + 2)
                tt(qa[:, :], ps[:, 0, :], cos[:, c], ALU.mult)
                mark(tt(qr[:, :], ps[:, 1, :], sin[:, c], ALU.mult), s["q_taken"], b + 1)
                if b >= 2:
                    dve.wait_ge(s["k_rows"][b % 2], 16 * NP * NP * (b // 2))
                if b:
                    dve.wait_ge(s["nq_mm"], b)
                link(tt(qa[:, :], qa[:, :], qr[:, :], ALU.add))
                cut_in_parts(qa[:, :], q3[:, b % 2], sq[:, 0, :]).then_inc(s["q_split"], 1)
                dve.wait_ge(s["sq_k"], b + 1)
                tt(sq[:, 2, :], q3[:, b % 2, 0, :], k3[:, b % 2, 0, :], ALU.mult).then_inc(s["sq_q"], 1)

            def take_key_norms(a, b):
                s = A[a]
                dve.wait_ge(s["nk_mm"], b + 1)
                mark(nc.vector.tensor_reduce(kmx[:, (b > 0):(b > 0) + 1], ps[0:H, 7, :], AX.X, ALU.max),
                     s["nk_max"], b + 1)
                if b:
                    link(tt(kmx[:, 0:1], kmx[:, 0:1], kmx[:, 1:2], ALU.max))

            def spread_key_norms(a, n):
                s = A[a]
                ts(kdg[:, :], ident[0:H, 0:H], kmx[:, 0:1], 1.03, ALU.mult, ALU.mult).then_inc(s["kdiag"], 1)
                dve.wait_ge(s["kmb_mm"], n)
                link(copy(kmb[:, :], ps[:, 7, 0:H]))

            def take_query_norms(a, b):
                s = A[a]
                tiles = slice(b * TB, (b + 1) * TB)
                v = ps[:, 6, 0:2 * TB * H].rearrange("p (n i h) -> p n i h", n=2, i=TB)
                dve.wait_ge(s["nq_mm"], b + 1)
                if a == 1:
                    copy(low[:, tiles, :], v[:, 1])
                mark(copy(nq[:, tiles, :], v[:, 0]), s["nq_taken"], b + 1)

            def shift(a, b0, b1, n):
                s = A[a]
                tiles = slice(b0 * TB, b1 * TB)
                q2, lo, u, c = nq[:, tiles, :], low[:, tiles, :], bound[:, tiles, :], shf[:, tiles, :]
                w = [(sw1 if a == 1 else sw2)[:, k] for k in range(3)]
                km = kmb[:, :].unsqueeze(1).to_broadcast([P, (b1 - b0) * TB, H])
                link(tt(u, q2, km, ALU.mult))
                link(ts(u, u, 1e-20, None, ALU.add))
                rsqrt(w[0], u, w[1], w[2], 2)
                link(tt(u, u, w[0], ALU.mult))
                mark(nc.vector.scalar_tensor_tensor(out=c, in0=u, scalar=-UNDER, in1=lo, op0=ALU.add, op1=ALU.max),
                     s["shift"], n)
                link(tt(u, u, lo, ALU.subtract))
                link(nc.vector.scalar_tensor_tensor(out=u, in0=q2, scalar=1e-10, in1=u, op0=ALU.mult, op1=ALU.max))
                link(nc.vector.scalar_tensor_tensor(out=u, in0=km, scalar=1e-10, in1=u, op0=ALU.mult, op1=ALU.max))
                link(ts(u, u, SPAN, None, ALU.is_le))
                link(nc.vector.tensor_reduce(oks[:, 0:1], u, AX.XY, ALU.min))
                ts(oks[:, 1:2], oks[:, 0:1], -1.0, 1.0, ALU.mult, ALU.add).then_inc(s["ok"], 1)

            def take_shift(a, b, n):
                s = A[a]
                dve.wait_ge(s["shiftT"], n)
                mark(ts(negc[:, b * BLK:(b + 1) * BLK], ps[0:H, 7, :], -1.0, None, ALU.mult), s["negc"], n)

            def take_ok(a, b0, b1, n):
                s = A[a]
                f = (a - 1) * NB
                dve.wait_ge(s["ok_mm"], n)
                mark(copy(flags[0:1, f + b0:f + b1], ps[0:1, 6, 0:1].to_broadcast([1, b1 - b0])), s["flag"], n)

            def general(a, qb):
                s = A[a]
                f = (a - 1) * NB + qb
                if qb:
                    dve.wait_ge(s["c_row"], 16 * qb)
                elif a == 2:
                    dve.wait_ge(A[1]["c_row"], 16 * NB)
                bad = dve.value_load(flags[0:1, f:f + 1], min_val=0, max_val=P)
                with dve.If(bad != 0):
                    dve.sem_inc(s["gen_f"][qb], 1)
                    with dve.Fori(0, H) as h:
                        for i in range(TB):
                            dve.wait_ge(s["gen_s"][qb], h * TB + i + 1)
                            to = mnat[:, i, bass.ds(h, 1)]
                            if a == 1:
                                at, seen = i * P, (h * TB + i) * 2
                                tt(masked[:, :], ps[:, qb, at:at + P], cmask[:, :], ALU.add)
                                flat = ps[:, :, :].rearrange("p b t -> p (b t)")
                                n = qb * BLK + at
                                if n:
                                    ins = nc.vector.tensor_reduce(mpart[:, 0:1], flat[:, 0:n], AX.X, ALU.max)
                                else:
                                    ins = nc.vector.memset(mpart[:, 0:1], -3e38)
                                mark(ins, s["gen_d"][qb], seen + 1)
                                mark(nc.vector.tensor_reduce(mpart[:, 1:2], masked[:, :], AX.X, ALU.max),
                                     s["gen_d"][qb], seen + 2)
                                tt(to, mpart[:, 0:1], mpart[:, 1:2], ALU.max).then_inc(s["gen_f"][qb], 1)
                            else:
                                nc.vector.tensor_reduce(to, ps[:, 0:4, :], AX.XY, ALU.max).then_inc(s["gen_f"][qb], 1)
                    dve.wait_ge(s["gen_s"][qb], H * TB + 1)
                    mark(ts(negc[:, qb * BLK:(qb + 1) * BLK], ps[0:H, 7, :], -1.0, None, ALU.mult),
                         s["gen_d"][qb], 2 * H * TB + 1 if a == 1 else 1)
                copy(negf[:, :], negc[:, qb * BLK:(qb + 1) * BLK]).then_inc(s["final"], 1)

            def evac(a, done):
                s = A[a]
                dve.wait_ge(s["pv"], RING + done)
                copy(accs[:, :], acc).then_inc(s["evac"], 1)

            def norm(a, n, g):
                s = A[a]
                dve.wait_ge(s["pt"], n + 1)
                v = psT.rearrange("p (i h c) -> p i h c", i=TB, h=HG)
                mark(nc.vector.reciprocal(rec[:, :, :], v[:, :, :, DK]), s["recip"], n + 1)
                o = att[:, :, bass.ds(g * HG * DK, HG * DK)].rearrange("p i (h d) -> p i h d", h=HG)
                tt(o, v[:, :, :, 0:DK], rec[:, :, :].unsqueeze(3).to_broadcast([P, TB, HG, DK]), ALU.mult
                   ).then_inc(s["norm"], 1)

            def post(a, qb):
                s = A[a]
                dve.wait_ge(s["post_t"], qb + 1)
                copy(attT[:, :], ps6).then_inc(s["post_e"], 1)
                dve.wait_ge(s["post_p"], qb + 1)
                xb = xn[:, qb * TB:(qb + 1) * TB, :]
                if a == 1 and qb == 0:
                    dve.wait_ge(ld_x, 16)
                mark(tt(xb if a == 1 else yb[:, :, :], xb, ps7r, ALU.add), s["post_x"], qb + 1)

            def rows_to_h(b):
                xb = xn[:, b * TB:(b + 1) * TB, :]
                link(layernorm(xb, xb))
                layernorm(zb, xb).then_inc(z, 1)

            def split2(b):
                s = A[2]
                dve.wait_ge(zT, b + 1)
                ts(hT[:, :], ps6, ln[:, 0:1], ln[:, 1:2], ALU.mult, ALU.add).then_inc(hTs, 1)
                dve.wait_ge(s["q_proj"], b + 1)
                mark(copy(qa[:, :], ps6), s["q_taken"], b + 1)
                dve.wait_ge(s["k_proj"], b + 1)
                mark(copy(ka[:, :], ps7), s["k_taken"], b + 1)
                if b >= 2:
                    dve.wait_ge(scratch_out, 16 * (2 * NB + 2 * (b - 1)))
                else:
                    dve.wait_ge(scratch_out, 16 * 2 * NB)
                dve.wait_ge(s["nk_mm"] if b else A[1]["nk_mm"], b if b else NB)
                dve.wait_ge(s["nq_mm"] if b else A[1]["nq_mm"], b if b else NB)
                link(copy(k3[:, b % 2, 0, :], ka[:, :]))
                tt(sq[:, 1, :], ka[:, :], ka[:, :], ALU.mult).then_inc(s["sq_k"], 1)
                link(copy(q3[:, b % 2, 0, :], qa[:, :]))
                mark(tt(sq[:, 0, :], qa[:, :], qa[:, :], ALU.mult), s["sq_q"], b + 1)
                dve.wait_ge(s["v_proj"], b + 1)
                copy(v2[:, b * TB:(b + 1) * TB, :, :], ps6.rearrange("p (i h d) -> p i h d", i=TB, h=H)
                     ).then_inc(s["v_taken"], 1)
                if b == 0:
                    tt(kblk[:, :].rearrange("p (h t) -> p h t", h=H),
                       k3[:, 0, 0, 0:NSUB].unsqueeze(1).to_broadcast([P, H, NSUB]),
                       blk[:, :].unsqueeze(2).to_broadcast([P, H, NSUB]), ALU.mult).then_inc(kbd, 1)
                for work, p3, done in ((ka, k3, "k_split"), (qa, q3, "q_split")):
                    link(tt(work[:, :], work[:, :], p3[:, b % 2, 0, :], ALU.subtract))
                    link(copy(p3[:, b % 2, 1, :], work[:, :]))
                    tt(p3[:, b % 2, 2, :], work[:, :], p3[:, b % 2, 1, :], ALU.subtract).then_inc(s[done], 1)
                take_key_norms(2, b)
                take_query_norms(2, b)
                for i in range(TB):
                    t = b * TB + i
                    dve.wait_ge(low_mm, t + 1)
                    mark(nc.vector.tensor_reduce(low[:, t, :], ps[:, 6:8, :].rearrange("p b (h t) -> p (b h) t", t=NSUB),
                                                 AX.X, ALU.max), low_taken, t + 1)

            def route(b):
                xb = xn[:, b * TB:(b + 1) * TB, :]
                if b:
                    dve.wait_ge(m_done, 16 * b)
                layernorm(zb, yb).then_inc(m_z, 1)
                dve.wait_ge(m_zT, b + 1)
                ts(hT[:, :], ps6, ln[:, 2:3], ln[:, 3:4], ALU.mult, ALU.add).then_inc(m_h, 1)
                link(tt(xb, xb, yb[:, :, :], ALU.add))
                dve.wait_ge(m_g, b + 1)
                link(tt(lg[:, :, :], ps[:, 7, 0:TB * E].rearrange("p (i e) -> p i e", i=TB),
                        gb[:, :].unsqueeze(1).to_broadcast([P, TB, E]), ALU.add))
                for i in range(TB):
                    ins = nc.vector.max(mx8[:, i, :], lg[:, i, :])
                link(ins)
                for i in range(TB):
                    ins = nc.vector.max_index(ix8[:, i, :], mx8[:, i, :], lg[:, i, :])
                link(ins)
                link(copy(ixf[:, :], ix8[:, :, 0]))
                for i in range(TB):
                    ins = ts(oh[:, i, :], iota[:, :], ixf[:, i:i + 1], None, ALU.is_equal)
                ins.then_inc(m_oh, 1)
                dve.wait_ge(m_ohT, b + 1)
                copy(ohT[:, :], ps[0:E, 7, :]).then_inc(m_ohTs, 1)

            def masks(b, e0, e1):
                for e in range(e0, e1):
                    dve.wait_ge(m_mk, b * E + e + 1)
                    mark(copy(ms[:, e, :], ps[:, 6 + e % 2, :]), m_ms, b * E + e + 1)

            def products(b, c):
                for k in range(c * E, (c + 1) * E, 2):
                    n = b * 2 * TB * E + k
                    if n >= PSLOTS:
                        dve.wait_ge(m_mm, n - PSLOTS + 1)
                    tt(prod[:, n % PSLOTS, :], hT[:, :] if c < TB else hid[:, c - TB, :], ms[:, k % E, :], ALU.mult
                       ).then_inc(m_pd, 1)

            def gelu_arg(b, c):
                dve.wait_ge(m_xh, b * TB + c + 1)
                x, t = hid[:, c, :], tg[:, c % 2, :]
                link(tt(t, x, x, ALU.mult))
                link(ts(t, t, 0.044715, 1.0, ALU.mult, ALU.add))
                tt(t, t, x, ALU.mult).then_inc(m_arg, 1)

            def gelu(b, c):
                dve.wait_ge(m_tanh, b * TB + c + 1)
                x, t = hid[:, c, :], tg[:, c % 2, :]
                mark(nc.vector.scalar_tensor_tensor(out=x, in0=t, scalar=1.0, in1=x, op0=ALU.add, op1=ALU.mult),
                     m_hid, b * TB + c + 1)

            def experts(b):
                products(b, 0)
                products(b, 1)
                gelu_arg(b, 0)
                products(b, 2)
                gelu(b, 0)
                gelu_arg(b, 1)
                products(b, 3)
                gelu(b, 1)
                gelu_arg(b, 2)
                products(b, TB)
                gelu(b, 2)
                gelu_arg(b, 3)
                products(b, TB + 1)
                gelu(b, 3)
                products(b, TB + 2)
                products(b, TB + 3)
                dve.wait_ge(m_mm, (b + 1) * 2 * TB * E)
                ts(yT[:, :], ps6, 0.5, None, ALU.mult).then_inc(m_yT, 1)

            def finish(b):
                xb = xn[:, b * TB:(b + 1) * TB, :]
                dve.wait_ge(m_yn, b + 1)
                link(tt(xb, xb, ps7r, ALU.add))
                layernorm(zb, xb).then_inc(m_out, 1)

            def attention(a):
                causal = a == 1
                general(a, 0)
                for qb in range(NB):
                    base, T = first_step(causal, qb), steps_of(causal, qb)
                    if qb:
                        norm(a, G * qb - 1, G - 1)
                        post(a, qb - 1)
                        if not causal:
                            route(qb - 1)
                            masks(qb - 1, 0, 6)
                    if qb + 1 < NB:
                        general(a, qb + 1)
                    evac(a, base + T)
                    if qb and not causal:
                        masks(qb - 1, 6, E)
                    if qb and causal:
                        rows_to_h(qb - 1)
                    norm(a, G * qb, 0)
                    if qb and causal:
                        split2(qb - 1)
                    if qb and not causal:
                        experts(qb - 1)
                    evac(a, base + 2 * T)
                    if qb and not causal:
                        finish(qb - 1)
                    with dve.Fori(UNROLLED, G) as g:
                        norm(a, G * qb + g - 1, g - 1)
                        evac(a, base + (g + 1) * T)
                norm(a, G * NB - 1, G - 1)
                post(a, NB - 1)

            nc.vector.memset(kaf[64:96, :], 0.0)
            nc.vector.memset(kaf[96:97, :], float(np.uint32(0x3F803F80).view(np.float32))).then_inc(init, 1)
            nc.vector.memset(onesf[:, :], 1.0)
            dve.wait_ge(ld_w, 32)
            copy(blk[:, :], blkf[:, :]).then_inc(init, 1)
            dve.wait_ge(init, 3)
            for b in range(NB):
                split1(b)
                take_key_norms(1, b)
                spread_key_norms(1, b + 1)
                take_query_norms(1, b)
                shift(1, b, b + 1, b + 1)
                take_shift(1, b, b + 1)
                take_ok(1, b, b + 1, b + 1)
            dve.wait_ge(ld_e, 16 * 11)
            copy(esel[:, :].rearrange("k (e p) -> k e p", e=E), ident[0:E, 0:E].unsqueeze(2).to_broadcast([E, E, P]))
            attention(1)
            b = NB - 1
            rows_to_h(b)
            split2(b)
            spread_key_norms(2, 1)
            shift(2, 0, NB, 1)
            for b in range(NB):
                take_shift(2, b, b + 1)
            take_ok(2, 0, NB, 1)
            attention(2)
            b = NB - 1
            route(b)
            masks(b, 0, E)
            experts(b)
            finish(b)


def kernel(**inputs):
    import concourse.bacc as _bacc
    from concourse.bass_utils import run_bass_kernel_spmd as _run

    def by_column(w, swapped=False):
        w = np.asarray(w).reshape(D, H, DK // 2, 2)
        return (w[:, :, :, ::-1] if swapped else w).reshape(D, H, DK).transpose(0, 2, 1).reshape(D, D)

    x = inputs["L0_attn_x"].reshape(S, D)
    wq = np.asarray(inputs["L0_attn_q_proj_weight"]).T
    wk = np.asarray(inputs["L0_attn_k_proj_weight"]).T
    wv = np.asarray(inputs["L0_attn_v_proj_weight"]).T
    wqkv = np.asarray(inputs["L0_ffn_w_qkv"])
    inv = (1.0 / THETA ** (np.arange(0, DK, 2, dtype=np.float32) / np.float32(DK))).astype(np.float32)
    ang = np.arange(S, dtype=np.float32)[None, :] * inv[:, None]
    c, s = np.cos(ang).astype(np.float32), np.sin(ang).astype(np.float32)
    cos = np.repeat(np.repeat(c, 2, axis=0), H, axis=0)
    sin = np.repeat(np.stack([-s, s], axis=1).reshape(DK, S), H, axis=0)
    p = np.arange(P)
    given = dict(
        xT=np.asarray(x).T, x=x, wa=np.concatenate([by_column(wq), by_column(wq, True), by_column(wk), by_column(wk, True), wv], axis=1),
        wo=np.asarray(inputs["L0_attn_o_proj_weight"]).T, wqkv=np.concatenate([by_column(wqkv[:, 0:D]), by_column(wqkv[:, D:2 * D]), wqkv[:, 2 * D:]], axis=1), wproj=inputs["L0_ffn_w_proj"],
        ln1w=inputs["L0_ffn_ln1_w"].reshape(D, 1), ln1b=inputs["L0_ffn_ln1_b"].reshape(D, 1),
        ln2w=inputs["L0_ffn_ln2_w"].reshape(D, 1), ln2b=inputs["L0_ffn_ln2_b"].reshape(D, 1),
        gw=inputs["L0_ffn_gate_w"], gb=np.tile(np.asarray(inputs["L0_ffn_gate_b"]).reshape(1, E), (P, 1)),
        w1=inputs["L0_ffn_w1"], w2=inputs["L0_ffn_w2"],
        cos=cos, sin=sin, ident=np.eye(P, dtype=np.float32),
        blk=(p[:, None] % H == np.arange(H)[None, :]).astype(np.float32),
        cmask=np.where(p[None, :] > p[:, None], -3e38, 0.0).astype(np.float32),
        iota=np.tile(np.arange(E, dtype=np.float32), (P, 1)),
    )
    nc = _bacc.Bacc("TRN2", target_bir_lowering=False, num_devices=1)
    arrays, args = {}, []
    for name, a in given.items():
        a = np.ascontiguousarray(a)
        arrays[f"in_{name}"] = a
        args.append(nc.dram_tensor(f"in_{name}", a.shape, mybir.dt.from_np(a.dtype), kind="ExternalInput").ap())
    out = nc.dram_tensor("out_0", (S, D), F32, kind="ExternalOutput").ap()
    build(nc, *args, out)
    r = _run(nc, [arrays], core_ids=[0])
    return r.results[0]["out_0"].reshape(1, S, D)
```

```python
from contextlib import ExitStack

import numpy as np

import concourse.bass as bass
from concourse import mybir

ALU = mybir.AluOpType
ACT = mybir.ActivationFunctionType
AX = mybir.AxisListType
F32 = mybir.dt.float32
BF16 = mybir.dt.bfloat16
U32 = mybir.dt.uint32
I32 = mybir.dt.int32

S = 2048
D = 128
H = 16
DK = D // H
E = 8
HID = 4 * D
EPS = 1e-5
THETA = 10000.0
P = 128

NP = 3
ROWS = NP * NP * DK
SHIFT_ROW = 96
KR = SHIFT_ROW + 1
BLK = 512
NB = S // BLK
TB = BLK // P
G = 4
HG = H // G
SCALE = float(1.0 / np.sqrt(DK))
VW = DK + 1
NSUB = 64
RING = 4

UNDER = 64.0 / SCALE
SPAN = 124.0 / SCALE


WSLOTS = 3
PSLOTS = 4
SIDE_FIRST, SIDE_LAST = 19, 31
PADW = 4096
TURN_STEP = 3
SHIFT_AT = (None, 4, 6, 8, 9)
UNROLLED = 2


def steps_of(causal, qb):
    return TB * (qb + 1) if causal else S // P


def first_step(causal, qb):
    return sum(G * steps_of(causal, b) for b in range(qb))


def ring_steps(causal, qb):
    return sum(1 + (G - UNROLLED) * steps_of(causal, b) for b in range(qb))


def pre_step(c):
    n, steps = 2 * TB * E, SIDE_LAST + 1 - SIDE_FIRST
    return next(k for k in range(steps) if n * (k + 1) // steps >= (c + 1) * E) + SIDE_FIRST - S // P


def build(nc, xT_d, x_d, wa_d, wo_d, wqkv_d, wproj_d, ln1w_d, ln1b_d, ln2w_d, ln2b_d, gw_d, gb_d,
          w1_d, w2_d, cos_d, sin_d, ident_d, blk_d, cmask_d, iota_d, pad_d, out_d):
    ctx = ExitStack()
    with ctx:
        def sb(name, shape, dt=F32):
            return ctx.enter_context(nc.sbuf_tensor(name, shape, dt))

        def sem(name):
            return ctx.enter_context(nc.semaphore(name))

        KA = sb("key_rows", [P, H * S], BF16)
        QA = sb("query_rows", [P, 2 * H * BLK], BF16)
        parts = sb("parts", [P, 4 * NP * BLK], BF16)
        q3 = parts[:, 0:2 * NP * BLK].rearrange("p (s j t) -> p s j t", s=2, j=NP)
        k3 = parts[:, 2 * NP * BLK:].rearrange("p (s j t) -> p s j t", s=2, j=NP)
        wring = parts[:, :].bitcast(F32).rearrange("p (s e n) -> p s e n", s=WSLOTS, e=E)
        V = sb("values", [P, (S // P) * H * VW])
        vring = sb("values_ring", [P, RING, HG, VW])
        Pr = sb("probs", [P, 2, HG, BLK])
        xn = sb("x_rows", [P, S // P, D])
        early = sb("early_late", [P, 3 * S])
        xT, cos, sin = (early[:, n * S:(n + 1) * S] for n in range(3))
        v2 = early[:, 0:S].rearrange("p (k h d) -> p k h d", k=S // P, h=H)
        hid = early[:, 0:S].rearrange("p (c t) -> p c t", c=TB)
        prod = early[:, S:2 * S].rearrange("p (c t) -> p c t", c=PSLOTS)
        ms = early[:, 2 * S:3 * S].bitcast(BF16).rearrange("p (e t) -> p e t", e=E)
        wa = sb("w_attn1", [P, 5 * D])
        wo = sb("w_out1", [P, D])
        wqkv = sb("w_attn2", [P, 3 * D])
        wproj = sb("w_out2", [P, D])
        qa = sb("q_work", [P, BLK])
        qr = sb("q_rotated", [P, BLK])
        ka = sb("k_work", [P, BLK])
        kr = sb("k_rotated", [P, BLK])
        accs, attT = qr, kr
        yT = qa
        sqk = sb("squares_blockdiag", [P, 3 * BLK + H * NSUB], BF16)
        sq = sqk[:, 0:3 * BLK].rearrange("p (n t) -> p n t", n=3)
        kblk = sqk[:, 3 * BLK:]
        tg = sqk[:, 0:4 * BLK].bitcast(F32).rearrange("p (n t) -> p n t", n=2)
        zb = sb("z_rows", [P, TB, D])
        att = sb("attn_rows", [P, TB, D])
        hT = sb("h_cols", [P, BLK])
        yb = wa[:, 0:TB * D].rearrange("p (i d) -> p i d", i=TB)
        ident = sb("ident", [P, P])
        blkf = sb("blk_f", [P, H])
        blk = sb("blk", [P, H], BF16)
        cmask = sb("cmask", [P, P])
        masked = sb("masked", [P, P])
        ln = sb("ln_wb", [P, 4])
        gw = sb("gate_w", [P, E])
        gb = sb("gate_b", [P, E])
        iota = sb("iota", [P, E])
        rec = sb("recip", [P, 2, TB, 2])
        mnat = sb("row_max", [P, TB, H])
        mpart = sb("row_max_parts", [P, 2])
        nq = sb("q_norms", [P, S // P, H])
        low = sb("row_low", [P, S // P, H])
        bound = sb("row_bound", [P, S // P, H])
        shf = sb("row_shift", [P, S // P, H])
        sw = [r.rearrange("p (k h) -> p k h", h=H) for r in (
            zb[:, 0:2, :].rearrange("p i d -> p (i d)"), zb[:, 2:4, :].rearrange("p i d -> p (i d)"), hT[:, 0:2 * D])]
        kmx = sb("k_norm_max", [H, 2])
        kdg = sb("k_norm_diag", [H, H])
        kmb = sb("k_norm_rows", [P, H])
        oks = sb("row_ok", [P, 2])
        negc = sb("neg_shift", [H, S], BF16)
        negf = sb("neg_shift_final", [H, BLK], BF16)
        onesf = sb("ones_f", [P, P])
        flags = sb("flags", [1, 4], I32)
        st = sb("ln_stats", [P, TB, 6])
        mv = sb("ln_meanvar", [P, TB, 2])
        nw = sb("ln_newton", [P, 7, TB])
        lg = sb("logits", [P, TB, E])
        mx8 = sb("logit_max", [P, TB, 8])
        ix8 = sb("logit_at", [P, TB, 8], U32)
        ixf = sb("logit_at_f", [P, TB])
        oh = sb("onehot", [P, TB, E])
        ohT = sb("onehot_T", [E, BLK], BF16)
        esel = sb("expert_rows", [E, E * P], BF16)
        k_scratch = nc.dram_tensor("k_scratch", (2, NP, DK, H, S), BF16, kind="Internal").ap()
        q_scratch = nc.dram_tensor("q_scratch", (2, NP, DK, H, S), BF16, kind="Internal").ap()

        ps = ctx.enter_context(nc.psum_tensor("ps", [P, 8, BLK], F32))

        def sums_bank(g):
            return ps[:, 4 + g % 2, :]

        ps6, ps7 = ps[:, 6, :], ps[:, 7, :]
        ps7r = ps7.rearrange("p (i d) -> p i d", i=TB)

        ld_a, ld_w, ld_x, ld_e, ld_pad = (sem(n) for n in ("ld_a", "ld_w", "ld_x", "ld_e", "ld_pad"))
        ld_b = [sem(f"ld_b{b}") for b in range(NB)]
        ld_m = [sem(f"ld_m{n}") for n in range(WSLOTS)]
        init, scratch_out = sem("init"), sem("scratch_out")
        dch, pch = sem("dve_chain"), sem("pool_chain")
        A = {}
        for a in (1, 2):
            s = {}
            for n in ("q_proj", "k_proj", "v_proj", "q_taken", "k_taken", "v_taken", "q_split", "k_split",
                      "sq_q", "sq_k", "nk_mm", "nk_max", "kdiag", "kmb_mm", "nq_mm", "nq_taken",
                      "shift", "shiftT", "negc", "ok", "ok_mm", "flag", "final",
                      "S", "exp", "pv", "v", "evac", "recip", "pt", "norm", "post_t", "post_e", "post_p",
                      "post_x"):
                s[n] = sem(f"a{a}_{n}")
            for n in ("gen_s", "gen_f", "gen_d"):
                s[n] = [sem(f"a{a}_{n}{b}") for b in range(NB)]
            for n in ("k_rows", "q_rows"):
                s[n] = [sem(f"a{a}_{n}{b}") for b in range(2)]
            s["c_row"] = sem(f"a{a}_c_row")
            A[a] = s
        dg_seen = sem("dg_seen")
        A[1]["dg"] = sem("a1_cut")
        for n in ("k_sum", "q_sum", "q_cut"):
            A[1][n] = sem(f"a1_{n}")
        k_early = sem("k_rows_early")
        z, zT, hTs, kbd, low_mm, low_taken, v_moved = (
            sem(n) for n in ("a2_z", "a2_zT", "a2_hT", "k_blockdiag_set", "low_mm", "low_taken", "v_moved"))
        m_z, m_zT, m_h, m_g, m_oh, m_ohT, m_ohTs = (sem(f"m_{n}") for n in ("z", "zT", "h", "g", "oh", "ohT", "ohTs"))
        m_mk, m_ms, m_pd, m_pp, m_mm, m_xh, m_arg, m_tanh, m_hid, m_yT, m_yn, m_out, m_done = (
            sem(f"m_{n}") for n in ("mask_mm", "mask", "prod_dve", "prod_pool", "mm", "pre_copied",
                                    "tanh_arg", "tanh", "hid", "yT", "yn", "out", "done"))

        def low_banks(b, i):
            return (6, 7) if b < NB - 1 or i == 0 else (2 * i - 2, 2 * i - 1)

        KAv = KA[:, :].rearrange("p (h t) -> p h t", h=H)
        QAv = QA[:, :].rearrange("p (s h t) -> p s h t", s=2, h=H)
        Vv = V[:, :].rearrange("p (k h w) -> p k h w", h=H, w=VW)
        kaf, qaf = KA[:, :].bitcast(F32), QA[:, :].bitcast(F32)

        block = ctx.enter_context(nc.Block())

        @block.sync
        def _(sp):
            sp.dma_start(wa[:, :], wa_d).then_inc(ld_a, 16)
            for b in range(NB):
                c = slice(b * BLK, (b + 1) * BLK)
                sp.dma_start(xT[:, c], xT_d[:, c]).then_inc(ld_b[b], 16)
                sp.dma_start(cos[:, c], cos_d[:, c]).then_inc(ld_b[b], 16)
                sp.dma_start(sin[:, c], sin_d[:, c]).then_inc(ld_b[b], 16)
                if b == 0:
                    for t, s in ((blkf, blk_d), (ident, ident_d)):
                        sp.dma_start(t[:, :], s).then_inc(ld_w, 16)
            for c in range(0, KA.shape[1] // 2, PADW):
                sp.dma_start(kaf[ROWS:KR, c:c + PADW], pad_d).then_inc(ld_pad, 16)
            for c in range(0, QA.shape[1] // 2, PADW):
                sp.dma_start(qaf[ROWS:SHIFT_ROW, c:c + PADW], pad_d[0:SHIFT_ROW - ROWS, :]).then_inc(ld_pad, 16)
            for t, s in ((cmask, cmask_d), (wo, wo_d), (wqkv, wqkv_d), (wproj, wproj_d), (gw, gw_d),
                         (iota, iota_d), (gb, gb_d)):
                sp.dma_start(t[:, :], s).then_inc(ld_e, 16)
            for n, s in enumerate((ln1w_d, ln1b_d, ln2w_d, ln2b_d)):
                sp.dma_start(ln[:, n:n + 1], s).then_inc(ld_e, 16)
            sp.dma_start(xn[:, :, :], x_d.rearrange("(t p) d -> p t d", p=P)).then_inc(ld_x, 16)

            parts_out = [0]

            def to_scratch(p3, scratch, b):
                sp.dma_start(scratch[:, :, :, b * BLK:(b + 1) * BLK].rearrange("j d h t -> (d h) j t"), p3
                             ).then_inc(scratch_out, 16)
                parts_out[0] += 16

            def scratch_written():
                sp.wait_ge(scratch_out, parts_out[0])

            def key_rows(a, heads, t0, t1, done):
                src = k_scratch[a - 1].rearrange("j d h t -> (j d) h t")
                for i in range(NP):
                    for j in range(NP):
                        r = (i * NP + j) * DK
                        sp.dma_start(KAv[r:r + DK, heads, t0:t1], src[i * DK:(i + 1) * DK, heads, t0:t1]
                                     ).then_inc(done, 16)

            def query_rows(a, b):
                src = q_scratch[a - 1, :, :, :, b * BLK:(b + 1) * BLK].rearrange("j d h t -> (j d) h t")
                for i in range(NP):
                    r = i * NP * DK
                    sp.dma_start(QAv[r:r + NP * DK, b % 2, :, :], src).then_inc(A[a]["q_rows"][b % 2], 16)

            def shift_row(a, b):
                sp.wait_ge(A[a]["final"], b + 1)
                sp.dma_start(QAv[SHIFT_ROW:SHIFT_ROW + 1, b % 2, :, :], negf[:, :]).then_inc(A[a]["c_row"], 16)

            def slot_free(a, b):
                if b >= 2:
                    sp.wait_ge(A[a]["S"], 2 * first_step(a == 1, b - 1))
                elif a == 2:
                    sp.wait_ge(A[1]["S"], 2 * first_step(True, NB - 1 + b))

            for b in range(NB):
                sp.wait_ge(A[1]["q_split"], b + 1)
                to_scratch(q3[:, b % 2], q_scratch[0], b)
                sp.wait_ge(A[1]["k_split"], b + 1)
                to_scratch(k3[:, b % 2], k_scratch[0], b)
                scratch_written()
                if b >= 2:
                    sp.wait_ge(A[1]["k_rows"][b % 2], 16 * NP * NP * (b // 2))
                key_rows(1, slice(0, H), b * BLK, (b + 1) * BLK, A[1]["k_rows"][b % 2])
                if b < 2:
                    query_rows(1, b)
            for qb in range(1, NB):
                shift_row(1, qb)
                if qb + 1 < NB:
                    slot_free(1, qb + 1)
                    query_rows(1, qb + 1)
                sp.wait_ge(A[2]["q_split"], qb)
                to_scratch(q3[:, (qb - 1) % 2], q_scratch[1], qb - 1)
                sp.wait_ge(A[2]["k_split"], qb)
                to_scratch(k3[:, (qb - 1) % 2], k_scratch[1], qb - 1)
            scratch_written()
            slot_free(2, 0)
            query_rows(2, 0)
            last = NB - 1
            for g in range(G):
                sp.wait_ge(A[1]["S"], 2 * (first_step(True, last) + (g + 1) * steps_of(True, last)))
                key_rows(2, slice(g * HG, (g + 1) * HG), 0, last * BLK, k_early)
            sp.wait_ge(A[2]["k_split"], NB)
            to_scratch(k3[:, last % 2], k_scratch[1], last)
            scratch_written()
            key_rows(2, slice(0, H), last * BLK, S, A[2]["k_rows"][0])
            sp.wait_ge(A[2]["q_split"], NB)
            to_scratch(q3[:, last % 2], q_scratch[1], last)
            slot_free(2, 1)
            query_rows(2, 1)
            scratch_written()

            def expert_weights(n):
                b, c = n // (2 * TB), n % (2 * TB)
                if n >= WSLOTS:
                    sp.wait_ge(m_mm, (n - WSLOTS + 1) * E)
                u = slice(c % TB * P, (c % TB + 1) * P)
                src = w1_d[:, :, u] if c < TB else w2_d[:, u, :]
                sp.dma_start(wring[:, n % WSLOTS], src.rearrange("e p n -> p e n")).then_inc(ld_m[n % WSLOTS], 16)

            def rows_out(b):
                sp.wait_ge(m_out, b + 1)
                sp.dma_start(out_d[b * BLK:(b + 1) * BLK, :].rearrange("(i p) d -> p i d", p=P), zb[:, :, :]
                             ).then_inc(m_done, 16)

            sp.wait_ge(low_mm, S // P)
            sp.wait_ge(A[2]["c_row"], 16)
            for n in range(WSLOTS):
                expert_weights(n)
            for qb in range(1, NB + 1):
                if qb < NB:
                    shift_row(2, qb)
                if qb + 1 < NB:
                    slot_free(2, qb + 1)
                    query_rows(2, qb + 1)
                for n in range(2 * TB):
                    n += (qb - 1) * 2 * TB + WSLOTS
                    if n < NB * 2 * TB:
                        expert_weights(n)
                rows_out(qb - 1)
            sp.wait_ge(m_done, 16 * NB)

        @block.tensor
        def _(pe):
            def mm(out, l, r, start=True, stop=True):
                return nc.tensor.matmul(out, l, r, start=start, stop=stop, skip_group_check=True)

            def turned(out, rows, m=P):
                for i in range(TB):
                    last = nc.tensor.transpose(out[0:m, i * P:(i + 1) * P], rows(i), ident[:, :])
                return last

            def project1(b):
                s = A[1]
                pe.wait_ge(ld_b[b], 48)
                src = xT[:, b * BLK:(b + 1) * BLK]
                for n in range(4):
                    name = "q" if n < 2 else "k"
                    pe.wait_ge(s[name + "_taken"], b)
                    mm(ps[:, n, :], wa[:, n * D:(n + 1) * D], src).then_inc(s[name + "_proj"], 1)
                pe.wait_ge(s["v_taken"], b)
                for i in range(TB):
                    last = mm(ps[:, 4, i * D:(i + 1) * D], src[:, i * P:(i + 1) * P], wa[:, 4 * D:5 * D])
                last.then_inc(s["v_proj"], 1)

            def project2(b):
                s = A[2]
                pe.wait_ge(hTs, b + 1)
                mm(ps7, wqkv[:, D:2 * D], hT[:, :]).then_inc(s["k_proj"], 1)
                mm(ps6, wqkv[:, 0:D], hT[:, :]).then_inc(s["q_proj"], 1)

            def project2_values(b):
                s = A[2]
                bank = 6 if b < NB - 1 else 5
                if bank == 6:
                    pe.wait_ge(s["q_taken"], b + 1)
                for i in range(TB):
                    last = mm(ps[:, bank, i * D:(i + 1) * D], hT[:, i * P:(i + 1) * P], wqkv[:, 2 * D:3 * D])
                last.then_inc(s["v_proj"], 1)

            def key_norms(a, b):
                s = A[a]
                if a == 1 and b == 0:
                    pe.wait_ge(init, 2)
                pe.wait_ge(s["sq_k"], b + 1)
                if a == 1:
                    pe.wait_ge(s["nk_max"], b)
                mm(ps[0:H, 7, :], blk[:, :], sq[:, 1, :]).then_inc(s["nk_mm"], 1)

            def key_bound(a):
                s = A[a]
                pe.wait_ge(s["kdiag"], 1)
                mm(ps[:, 7, 0:H], onesf[0:H, :], kdg[:, :]).then_inc(s["kmb_mm"], 1)

            def query_norms(a, b):
                s = A[a]
                pe.wait_ge(s["sq_q"], b + 1)
                pe.wait_ge(s["v_taken" if a == 2 else "nq_taken"], b + (a == 2))
                for n in range(2 if a == 1 else 1):
                    for i in range(TB):
                        at = (n * TB + i) * H
                        last = mm(ps[:, 6, at:at + H], sq[:, 2 * n, i * P:(i + 1) * P], blk[:, :])
                last.then_inc(s["nq_mm"], 1)

            def lows(b, i):
                t = b * TB + i
                if t == 0:
                    pe.wait_ge(kbd, 1)
                pe.wait_ge(A[2]["nq_taken"], b + 1)
                pe.wait_ge(low_taken, min(t, (NB - 1) * TB))
                for c in range(H * NSUB // BLK):
                    last = mm(ps[:, low_banks(b, i)[c], :], q3[:, b % 2, 0, i * P:(i + 1) * P], kblk[:, c * BLK:(c + 1) * BLK])
                last.then_inc(low_mm, 1)

            def shift_turn(a, b):
                s = A[a]
                pe.wait_ge(s["shift"], 1 + (b > 0))
                if b:
                    pe.wait_ge(s["negc"], b)
                turned(ps7, lambda i: shf[:, b * TB + i, :], H).then_inc(s["shiftT"], 1)

            def count_ok(a, n):
                s = A[a]
                pe.wait_ge(s["ok"], n)
                if n == 2:
                    pe.wait_ge(s["flag"], 1)
                mm(ps[0:1, 6, 0:1], oks[:, 1:2], onesf[:, 0:1]).then_inc(s["ok_mm"], 1)

            def settle(a):
                key_bound(a)
                shift_turn(a, 0)
                count_ok(a, 1)

            def keys_there(a, qb):
                if a == 1 and qb == 0:
                    pe.wait_ge(ld_pad, 16 * (H * S + 2 * H * BLK) // 2 // PADW)
                if a == 1:
                    pe.wait_ge(A[1]["k_rows"][qb % 2], 16 * NP * NP * (qb // 2 + 1))
                elif qb == 0:
                    pe.wait_ge(k_early, 16 * NP * NP * G)
                    pe.wait_ge(A[2]["k_rows"][0], 16 * NP * NP)

            def general(a, qb, base):
                s = A[a]
                f = 2 * (a - 1) + (qb > 0)
                pe.wait_ge(s["flag"], 1 + (qb > 0))
                bad = pe.value_load(flags[0:1, f:f + 1], min_val=0, max_val=P)
                with pe.If(bad != 0):
                    keys_there(a, qb)
                    pe.wait_ge(s["q_rows"][qb % 2], 16 * NP * (qb // 2 + 1))
                    pe.wait_ge(s["exp"], 2 * base + 2)
                    with pe.Fori(0, H) as h:
                        for i in range(TB):
                            nk = qb * BLK + (i + 1) * P if a == 1 else S
                            pe.wait_ge(s["gen_f"][qb], h * TB + i + 1)
                            for c in range(0, nk, BLK):
                                n = min(BLK, nk - c)
                                last = mm(ps[:, c // BLK, 0:n],
                                          QA[0:ROWS, bass.ds(h * BLK + (qb % 2) * H * BLK + i * P, P)],
                                          KA[0:ROWS, bass.ds(h * S + c, n)])
                            last.then_inc(s["gen_s"][qb], 1)
                    pe.wait_ge(s["gen_f"][qb], H * TB + 1)
                    turned(ps7, lambda i: mnat[:, i, :], H).then_inc(s["gen_s"][qb], 1)
                    pe.wait_ge(s["gen_d"][qb], 2 * H * TB + 1 if a == 1 else 1)

            def scores(s, slot, g, kt_at, t, lo, p):
                pe.wait_ge(s["exp"], 2 * t + p + 1)
                for hh in range(2):
                    h = g * HG + 2 * p + hh
                    last = mm(ps[:, 2 * p + hh, lo:BLK], KA[0:KR, bass.ds(h * S + kt_at, P)],
                              QA[0:KR, bass.ds(h * BLK + slot * H * BLK + lo, BLK - lo)])
                last.then_inc(s["S"], 1)

            def values(a, step, n, p):
                s = A[a]
                t, i, lo = step["t"], step["i"], step["lo"] // P
                if step["ring"] is not None and p == 0:
                    pe.wait_ge(s["v"], step["ring"])
                pe.wait_ge(s["exp"], 2 * t + p + 3)
                if step["cut"] is not None:
                    pe.wait_ge(s["dg"], step["cut"] + p)
                if step["start"] and p == 0 and n >= 2:
                    pe.wait_ge(s["norm"], n - 1)
                out = step["bank"]
                for odd in range(2):
                    first = max(0, (lo - odd + 1) // 2)
                    if first > 1:
                        continue
                    for hh in range(2):
                        h = 2 * p + hh
                        at = 32 * (2 * odd + hh)
                        w = vring[:, i, h, :] if step["ring"] is not None else Vv[:, step["kt"], step["g"] * HG + h, :]
                        src = Pr[:, i % 2, h, :].rearrange("k (j o q) -> k j o q", o=2, q=P)[:, first:, odd, :]
                        last = mm(out[at:at + VW, 2 * p * P + first * P:2 * (p + 1) * P], w, src,
                                  start=step["start"] and p == 0, stop=step["stop"])
                last.then_inc(s["pv"], 1)

            def turn(a, n, bank):
                s = A[a]
                pe.wait_ge(s["evac"], n + 1)
                turned(bank, lambda i: accs[:, i * P:(i + 1) * P]).then_inc(s["pt"], 1)

            def post_turn(a, qb):
                s = A[a]
                pe.wait_ge(s["norm"], G * (qb + 1))
                turned(ps6, lambda i: att[:, i, :]).then_inc(s["post_t"], 1)

            def post_project(a, qb):
                s = A[a]
                pe.wait_ge(s["post_e"], qb + 1)
                for i in range(TB):
                    last = mm(ps[:, 7, i * D:(i + 1) * D], attT[:, i * P:(i + 1) * P], (wo if a == 1 else wproj)[:, :])
                last.then_inc(s["post_p"], 1)

            def z_turn(b):
                pe.wait_ge(z, b + 1)
                turned(ps6, lambda i: zb[:, i, :]).then_inc(zT, 1)

            def m_turn(b):
                pe.wait_ge(m_z, b + 1)
                turned(ps6, lambda i: zb[:, i, :]).then_inc(m_zT, 1)

            def m_gate(b):
                pe.wait_ge(m_h, b + 1)
                for i in range(TB):
                    last = mm(ps[:, 7, i * E:(i + 1) * E], hT[:, i * P:(i + 1) * P], gw[:, :])
                last.then_inc(m_g, 1)

            def m_onehot(b):
                pe.wait_ge(m_oh, b + 1)
                turned(ps7, lambda i: oh[:, i, :], E).then_inc(m_ohT, 1)

            def m_masks(b, e0, e1):
                pe.wait_ge(m_ohTs, b + 1)
                for e in range(e0, e1):
                    pe.wait_ge(m_ms, b * E + max(0, e - 1))
                    mm(ps[:, 6 + e % 2, :], esel[:, e * P:(e + 1) * P], ohT[:, :]).then_inc(m_mk, 1)

            def m_products(b, k0, k1):
                for k in range(k0, k1):
                    n = b * 2 * TB * E + k
                    c, e = k // E, k % E
                    if e == 0:
                        ch = n // E
                        pe.wait_ge(ld_m[ch % WSLOTS], 16 * (ch // WSLOTS + 1))
                        if c == 0:
                            pe.wait_ge(m_ms, (b + 1) * E)
                        if 2 <= c < TB:
                            pe.wait_ge(m_xh, b * TB + c - 1)
                        if c == TB:
                            pe.wait_ge(m_xh, b * TB + TB - 1)
                    pe.wait_ge(m_pd if n % 2 == 0 else m_pp, n // 2 + 1)
                    if c < TB:
                        out, start, stop = ps[:, 6 + c % 2, :], e == 0, e == E - 1
                    else:
                        out, start, stop = ps6, k == TB * E, k == 2 * TB * E - 1
                    mm(out, wring[:, (n // E) % WSLOTS, e, :], prod[:, n % PSLOTS, :], start, stop).then_inc(m_mm, 1)

            def m_back(b):
                pe.wait_ge(m_yT, b + 1)
                turned(ps7, lambda i: yT[:, i * P:(i + 1) * P]).then_inc(m_yn, 1)

            def group(a, qb, g, n, pending, side):
                s = A[a]
                causal = a == 1
                T = steps_of(causal, qb)
                t0 = first_step(causal, qb) + g * T
                full = qb if causal else NB
                looped = g >= UNROLLED
                ring0 = ring_steps(causal, qb) + 1 + (g - UNROLLED) * T if looped else None
                g_last = not looped and g == UNROLLED - 1

                def step(kb, i, diag, opening):
                    nonlocal pending
                    lo = i * P if diag else 0
                    at = kb * TB + i
                    for p in range(2):
                        scores(s, qb % 2, g, kb * BLK + i * P, t0 + at, lo, p)
                        if pending is not None:
                            values(a, pending, n, p)
                    pending = dict(t=t0 + at, i=i, lo=lo, g=g, bank=sums_bank(g), kt=at, ring=ring0 + at + 1 if looped else None,
                                   cut=2 * (n * TB + i) + 1 if diag else None, start=opening and i == 0, stop=False)
                    if opening and i == TURN_STEP and n:
                        turn(a, n - 1, sums_bank(g - 1))
                    for f in side.get(at, ()) if isinstance(kb, int) else ():
                        f()

                def steps(kb, diag, opening):
                    for i in range(TB):
                        step(kb, i, diag, opening)

                steps(0, full == 0, True)
                if full > 1:
                    if looped:
                        t_in, r_in = t0 + TB - 1, ring0 + TB
                        with pe.Fori(1, full) as kb:
                            pending = dict(pending, t=t_in + (kb - 1) * TB, ring=r_in + (kb - 1) * TB)
                            steps(kb, False, False)
                        pending = dict(pending, t=t0 + full * TB - 1, ring=ring0 + full * TB)
                    else:
                        for kb in range(1, full):
                            steps(kb, False, False)
                if causal and full > 0:
                    steps(full, True, False)
                return dict(pending, stop=True, **({"ring": ring_steps(causal, qb) + 1} if g_last else {}))

            def attention(a, side):
                causal = a == 1
                s = A[a]
                general(a, 0, 0)
                pending = None
                for qb in range(NB):
                    base, T = first_step(causal, qb), steps_of(causal, qb)
                    keys_there(a, qb)
                    if not causal and qb == 0:
                        pe.wait_ge(v_moved, 1)
                    pe.wait_ge(s["q_rows"][qb % 2], 16 * NP * (qb // 2 + 1))
                    pe.wait_ge(s["c_row"], 16 * (qb + 1))
                    todo = side(qb)
                    for g in range(G):
                        here = {p - g * T: f for p, f in todo.items() if g * T <= p < (g + 1) * T}
                        if g == G - 1 and qb + 1 < NB:
                            general(a, qb + 1, base + (G - 1) * T)
                        pending = group(a, qb, g, G * qb + g, pending, here)
                for p in range(2):
                    values(a, pending, 0, p)
                turn(a, G * NB - 1, sums_bank(G - 1))

            def side0(a):
                todo = {SHIFT_AT[b]: [lambda b=b: shift_turn(a, b)] for b in range(1, NB)}
                todo[SHIFT_AT[NB]] = [lambda: count_ok(a, 2)]
                return todo

            def side1(qb):
                if qb == 0:
                    return side0(1)
                b = qb - 1
                todo = {5: [lambda: post_turn(1, b)], 7: [lambda: post_project(1, b)], 14: [lambda: z_turn(b)],
                        16: [lambda: project2(b)], 18: [lambda: project2_values(b)],
                        20: [lambda: key_norms(2, b), lambda: query_norms(2, b)]}
                for i in range(TB):
                    todo[21 + i] = [lambda i=i: lows(b, i)]
                return todo

            def side2(qb):
                if qb == 0:
                    return side0(2)
                b = qb - 1
                todo = {5: [lambda: post_turn(2, b)], 7: [lambda: post_project(2, b)], 10: [lambda: m_turn(b)],
                        11: [lambda: m_gate(b)], 13: [lambda: m_onehot(b)]}
                for e in range(0, E, 2):
                    todo[14 + e // 2] = [lambda e=e: m_masks(b, e, e + 2)]
                first, last, n = SIDE_FIRST, SIDE_LAST, 2 * TB * E
                cuts = [n * k // (last + 1 - first) for k in range(last + 2 - first)]
                for k in range(last + 1 - first):
                    todo.setdefault(first + k, []).append(lambda k=k: m_products(b, cuts[k], cuts[k + 1]))
                todo[33] = [lambda: m_back(b)]
                return todo

            pe.wait_ge(ld_a, 16)
            for b in range(NB + 1):
                if b < NB:
                    project1(b)
                if b:
                    key_norms(1, b - 1)
                    query_norms(1, b - 1)
            settle(1)
            attention(1, side1)
            b = NB - 1
            post_turn(1, b)
            post_project(1, b)
            z_turn(b)
            project2(b)
            project2_values(b)
            key_norms(2, b)
            query_norms(2, b)
            for i in range(TB):
                lows(b, i)
            settle(2)
            attention(2, side2)
            b = NB - 1
            post_turn(2, b)
            post_project(2, b)
            m_turn(b)
            m_gate(b)
            m_onehot(b)
            m_masks(b, 0, E)
            m_products(b, 0, 2 * TB * E)
            m_back(b)

        @block.scalar
        def _(act):
            def exps(a, t, i, lo):
                s = A[a]
                for p in range(2):
                    act.wait_ge(s["pv"], 2 * t + p + 5)
                    act.wait_ge(s["S"], 2 * t + p + 1)
                    nc.scalar.activation(Pr[:, i % 2, 2 * p:2 * p + 2, lo:BLK], ps[:, 2 * p:2 * p + 2, lo:BLK],
                                         ACT.Exp, scale=SCALE).then_inc(s["exp"], 1)

            def group(a, qb, g, side):
                causal = a == 1
                full = qb if causal else NB
                t0 = first_step(causal, qb) + g * steps_of(causal, qb)

                def steps(kb, diag):
                    for i in range(TB):
                        exps(a, t0 + kb * TB + i, i, i * P if diag else 0)
                        if isinstance(kb, int):
                            for f in side.get(kb * TB + i, ()):
                                f()

                if full and isinstance(g, int) and side:
                    for kb in range(full):
                        steps(kb, False)
                elif full:
                    with act.Fori(0, full) as kb:
                        steps(kb, False)
                if causal:
                    steps(full, True)

            def pre_copy(b, c):
                act.wait_ge(m_mm, b * 2 * TB * E + (c + 1) * E)
                nc.scalar.activation(hid[:, c, :], ps[:, 6 + c % 2, :], ACT.Copy).then_inc(m_xh, 1)

            def tanh(b, c):
                act.wait_ge(m_arg, b * TB + c + 1)
                nc.scalar.activation(tg[:, c % 2, :], tg[:, c % 2, :], ACT.Tanh,
                                     scale=float(np.sqrt(2.0 / np.pi))).then_inc(m_tanh, 1)

            def first_shift_row(a):
                act.wait_ge(A[a]["final"], 1)
                act.dma_start(QAv[SHIFT_ROW:SHIFT_ROW + 1, 0, :, :], negf[:, :]).then_inc(A[a]["c_row"], 16)

            def first_parts(b, name, work, p3, n):
                s = A[1]
                act.wait_ge(s[name + "_sum"], b + 1)
                if b >= 2:
                    act.wait_ge(scratch_out, 16 * 2 * (b - 1))
                if b:
                    act.wait_ge(s[f"n{name}_mm"], b)
                nc.scalar.activation(p3[:, b % 2, 0, :], work[:, :], ACT.Copy)
                nc.scalar.activation(sq[:, n, :], work[:, :], ACT.Square).then_inc(s["sq_k" if n else "q_cut"], 1)

            act.wait_ge(init, 2)
            for b in range(NB):
                first_parts(b, "k", ka, k3, 1)
                first_parts(b, "q", qa, q3, 0)
                act.wait_ge(A[1]["v_proj"], b + 1)
                nc.scalar.activation(Vv[:, b * TB:(b + 1) * TB, :, 0:DK],
                                     ps[:, 4, :].rearrange("p (i h d) -> p i h d", i=TB, h=H),
                                     ACT.Copy).then_inc(A[1]["v_taken"], 1)
            first_shift_row(1)
            for qb in range(NB):
                with act.Fori(0, G) as g:
                    group(1, qb, g, {})
            b, s = NB - 1, A[2]
            act.wait_ge(s["q_proj"], NB)
            act.wait_ge(scratch_out, 16 * (2 * NB + 2 * (b - 1)))
            act.wait_ge(s["nq_mm"], b)
            nc.scalar.activation(q3[:, b % 2, 0, :], ps6, ACT.Copy)
            nc.scalar.activation(sq[:, 0, :], ps6, ACT.Square).then_inc(s["sq_q"], 1)
            act.wait_ge(s["q_split"], b)
            nc.scalar.activation(qa[:, :], ps6, ACT.Copy).then_inc(s["q_taken"], 1)
            act.wait_ge(s["v_proj"], NB)
            nc.scalar.activation(v2[:, b * TB:(b + 1) * TB, :, :],
                                 ps[:, 5, :].rearrange("p (i h d) -> p i h d", i=TB, h=H),
                                 ACT.Copy).then_inc(s["v_taken"], 1)
            first_shift_row(2)
            for qb in range(NB):
                if qb == 0:
                    with act.Fori(0, G) as g:
                        group(2, qb, g, {})
                else:
                    b = qb - 1
                    group(2, qb, 0, {})
                    side = {}
                    for c in range(TB):
                        side.setdefault(pre_step(c), []).append(lambda c=c: pre_copy(b, c))
                        side.setdefault(pre_step(c) + 1, []).append(lambda c=c: tanh(b, c))
                    group(2, qb, 1, side)
                    with act.Fori(2, G) as g:
                        group(2, qb, g, {})
            b = NB - 1
            for c in range(TB):
                pre_copy(b, c)
                if c:
                    tanh(b, c - 1)
            tanh(b, TB - 1)

        @block.gpsimd
        def _(pool):
            chain = [0]

            def link(ins):
                chain[0] += 1
                ins.then_inc(pch, 1)
                pool.wait_ge(pch, chain[0])

            def split_k(b):
                s = A[1]
                pool.wait_ge(s["k_taken"], b + 1)
                nc.gpsimd.tensor_tensor(ka[:, :], ka[:, :], kr[:, :], ALU.add).then_inc(s["k_sum"], 1)
                kk = k3[:, b % 2]
                pool.wait_ge(s["sq_k"], b + 1)
                link(nc.gpsimd.tensor_tensor(ka[:, :], ka[:, :], kk[:, 0, :], ALU.subtract))
                link(nc.gpsimd.tensor_copy(kk[:, 1, :], ka[:, :]))
                nc.gpsimd.tensor_tensor(kk[:, 2, :], ka[:, :], kk[:, 1, :], ALU.subtract).then_inc(s["k_split"], 1)

            def cut(t, i):
                s = A[1]
                for p in range(2):
                    pool.wait_ge(s["exp"], 2 * t + p + 3)
                    pool.sem_inc(dg_seen, 1)
                    at = Pr[:, i % 2, 2 * p:2 * p + 2, i * P:(i + 1) * P]
                    nc.gpsimd.affine_select(out=at, in_=at, compare_op=ALU.is_ge, fill=0.0, base=0,
                                            pattern=[[0, 2], [1, P]], channel_multiplier=-1).then_inc(s["dg"], 1)

            def group(a, qb, g, ring):
                s = A[a]
                causal = a == 1
                full = qb if causal else NB
                t0 = first_step(causal, qb) + g * steps_of(causal, qb)

                def copy_in(kb, i):
                    t = t0 + kb * TB + i
                    pool.wait_ge(s["pv"], 2 * t + 2)
                    nc.gpsimd.tensor_copy(
                        vring[:, i, :, :],
                        V[:, bass.ds((kb * TB + i) * H * VW + g * HG * VW, HG * VW)].rearrange(
                            "p (h w) -> p h w", h=HG)).then_inc(s["v"], 1)

                def steps(kb, diag):
                    for i in range(TB):
                        if ring:
                            copy_in(kb, i)
                        if diag:
                            cut(t0 + kb * TB + i, i)

                if full and ring:
                    with pool.Fori(0, full) as kb:
                        steps(kb, False)
                if causal:
                    steps(full, True)
                if not ring and g == UNROLLED - 1:
                    copy_in(steps_of(causal, qb) // TB - 1, TB - 1)

            def products(b, k0, k1):
                for k in range(k0, k1):
                    n = b * 2 * TB * E + k
                    if n % 2 == 0:
                        continue
                    c, e = k // E, k % E
                    if k == 1:
                        pool.wait_ge(m_ms, (b + 1) * E)
                    if n >= PSLOTS:
                        pool.wait_ge(m_mm, n - PSLOTS + 1)
                    if c >= TB:
                        pool.wait_ge(m_hid, b * TB + c - TB + 1)
                    nc.gpsimd.tensor_tensor(prod[:, n % PSLOTS, :], hT[:, :] if c < TB else hid[:, c - TB, :],
                                            ms[:, e, :], ALU.mult).then_inc(m_pp, 1)

            link(nc.gpsimd.memset(V[:, :], 1.0))
            nc.gpsimd.memset(oks[:, :], 0.0).then_inc(init, 1)
            for a in (1, 2):
                pool.sem_inc(A[a]["pv"], 2 * RING)
                pool.sem_inc(A[a]["exp"], 2)
            for b in range(NB):
                split_k(b)
            for b in range(NB):
                pool.wait_ge(A[1]["v_taken"], b + 1)
            for a in (1, 2):
                causal = a == 1
                if a == 2:
                    pool.wait_ge(A[1]["pv"], 2 * (RING + first_step(True, NB)))
                    b = NB - 1
                    pool.wait_ge(A[2]["q_taken"], NB)
                    link(nc.gpsimd.tensor_tensor(qa[:, :], qa[:, :], q3[:, b % 2, 0, :], ALU.subtract))
                    link(nc.gpsimd.tensor_copy(q3[:, b % 2, 1, :], qa[:, :]))
                    nc.gpsimd.tensor_tensor(q3[:, b % 2, 2, :], qa[:, :], q3[:, b % 2, 1, :], ALU.subtract
                                            ).then_inc(A[2]["q_split"], 1)
                    pool.wait_ge(A[2]["v_taken"], NB)
                    nc.gpsimd.tensor_copy(Vv[:, :, :, 0:DK], v2).then_inc(v_moved, 1)
                    pool.wait_ge(v_moved, 1)
                for qb in range(NB):
                    if not causal and qb:
                        products(qb - 1, 0, 2 * TB * E)
                    for g in range(UNROLLED):
                        group(a, qb, g, False)
                    with pool.Fori(UNROLLED, G) as g:
                        group(a, qb, g, True)
            products(NB - 1, 0, 2 * TB * E)

        @block.vector
        def _(dve):
            chain = [0]

            def link(ins):
                chain[0] += 1
                ins.then_inc(dch, 1)
                dve.wait_ge(dch, chain[0])

            tt, ts, copy = nc.vector.tensor_tensor, nc.vector.tensor_scalar, nc.vector.tensor_copy

            def mark(ins, s, n):
                ins.then_inc(s, 1)
                dve.wait_ge(s, n)

            def rsqrt(y, v, h, t, turns):
                link(ts(y.bitcast(I32), v.bitcast(I32), -0.5, 1597463007.0, ALU.mult, ALU.add))
                link(ts(h, v, -0.5, None, ALU.mult))
                for _ in range(turns):
                    link(tt(t, y, y, ALU.mult))
                    link(tt(t, t, h, ALU.mult))
                    link(nc.vector.scalar_tensor_tensor(out=y, in0=t, scalar=1.5, in1=y, op0=ALU.add, op1=ALU.mult))

            def layernorm(dst, src):
                for i in range(TB):
                    ins = nc.vector.bn_stats(st[:, i, :], src[:, i, :])
                link(ins)
                for i in range(TB):
                    ins = nc.vector.bn_aggr(mv[:, i, :], st[:, i, :])
                link(ins)
                v, y, h, t = (nw[:, n, :] for n in range(4))
                link(ts(v, mv[:, :, 1], EPS, None, ALU.add))
                rsqrt(y, v, h, t, 3)
                for i in range(TB):
                    ins = ts(dst[:, i, :], src[:, i, :], mv[:, i, 0:1], nw[:, 1, i:i + 1], ALU.subtract, ALU.mult)
                return ins

            def split1(b):
                s = A[1]
                c = slice(b * BLK, (b + 1) * BLK)
                dve.wait_ge(ld_b[b], 48)
                dve.wait_ge(s["k_proj"], 2 * b + 2)
                dve.wait_ge(s["k_split"], b)
                tt(ka[:, :], ps[:, 2, :], cos[:, c], ALU.mult)
                tt(kr[:, :], ps[:, 3, :], sin[:, c], ALU.mult).then_inc(s["k_taken"], 1)
                dve.wait_ge(s["q_proj"], 2 * b + 2)
                dve.wait_ge(s["q_split"], b)
                tt(qa[:, :], ps[:, 0, :], cos[:, c], ALU.mult)
                mark(tt(qr[:, :], ps[:, 1, :], sin[:, c], ALU.mult), s["q_taken"], b + 1)
                tt(qa[:, :], qa[:, :], qr[:, :], ALU.add).then_inc(s["q_sum"], 1)
                if b:
                    take_key_norms(1, b - 1)
                    take_query_norms(1, b - 1)
                dve.wait_ge(s["q_cut"], b + 1)
                link(tt(qa[:, :], qa[:, :], q3[:, b % 2, 0, :], ALU.subtract))
                link(copy(q3[:, b % 2, 1, :], qa[:, :]))
                tt(q3[:, b % 2, 2, :], qa[:, :], q3[:, b % 2, 1, :], ALU.subtract).then_inc(s["q_split"], 1)
                dve.wait_ge(s["sq_k"], b + 1)
                tt(sq[:, 2, :], q3[:, b % 2, 0, :], k3[:, b % 2, 0, :], ALU.mult).then_inc(s["sq_q"], 1)

            def take_key_norms(a, b):
                s = A[a]
                dve.wait_ge(s["nk_mm"], b + 1)
                mark(nc.vector.tensor_reduce(kmx[:, (b > 0):(b > 0) + 1], ps[0:H, 7, :], AX.X, ALU.max),
                     s["nk_max"], b + 1)
                if b:
                    link(tt(kmx[:, 0:1], kmx[:, 0:1], kmx[:, 1:2], ALU.max))

            def spread_key_norms(a):
                s = A[a]
                ts(kdg[:, :], ident[0:H, 0:H], kmx[:, 0:1], 1.03, ALU.mult, ALU.mult).then_inc(s["kdiag"], 1)
                dve.wait_ge(s["kmb_mm"], 1)
                link(copy(kmb[:, :], ps[:, 7, 0:H]))

            def take_query_norms(a, b):
                s = A[a]
                tiles = slice(b * TB, (b + 1) * TB)
                v = ps[:, 6, 0:2 * TB * H].rearrange("p (n i h) -> p n i h", n=2, i=TB)
                dve.wait_ge(s["nq_mm"], b + 1)
                if a == 1:
                    copy(low[:, tiles, :], v[:, 1])
                mark(copy(nq[:, tiles, :], v[:, 0]), s["nq_taken"], b + 1)

            def shift(a, b0, b1):
                s = A[a]
                n = 1 + (b0 > 0)
                tiles = slice(b0 * TB, b1 * TB)
                q2, lo, u, c = nq[:, tiles, :], low[:, tiles, :], bound[:, tiles, :], shf[:, tiles, :]
                w = [sw[k][:, 0:(b1 - b0) * TB, :] for k in range(3)]
                km = kmb[:, :].unsqueeze(1).to_broadcast([P, (b1 - b0) * TB, H])
                link(tt(u, q2, km, ALU.mult))
                link(ts(u, u, 1e-20, None, ALU.add))
                rsqrt(w[0], u, w[1], w[2], 2)
                link(tt(u, u, w[0], ALU.mult))
                mark(nc.vector.scalar_tensor_tensor(out=c, in0=u, scalar=-UNDER, in1=lo, op0=ALU.add, op1=ALU.max),
                     s["shift"], n)
                link(tt(u, u, lo, ALU.subtract))
                link(nc.vector.scalar_tensor_tensor(out=u, in0=q2, scalar=1e-10, in1=u, op0=ALU.mult, op1=ALU.max))
                link(nc.vector.scalar_tensor_tensor(out=u, in0=km, scalar=1e-10, in1=u, op0=ALU.mult, op1=ALU.max))
                link(ts(u, u, SPAN, None, ALU.is_le))
                link(nc.vector.tensor_reduce(oks[:, 0:1], u, AX.XY, ALU.min))
                ts(oks[:, 1:2], oks[:, 0:1], -1.0, 1.0, ALU.mult, ALU.add).then_inc(s["ok"], 1)

            def take_shift(a, b):
                s = A[a]
                dve.wait_ge(s["shiftT"], b + 1)
                mark(ts(negc[:, b * BLK:(b + 1) * BLK], ps[0:H, 7, :], -1.0, None, ALU.mult), s["negc"], b + 1)

            def take_ok(a, n):
                s = A[a]
                dve.wait_ge(s["ok_mm"], n)
                f = 2 * (a - 1) + n - 1
                mark(copy(flags[0:1, f:f + 1], ps[0:1, 6, 0:1]), s["flag"], n)

            def settle(a):
                spread_key_norms(a)
                shift(a, 0, 1)
                take_shift(a, 0)
                take_ok(a, 1)

            def general(a, qb):
                s = A[a]
                f = 2 * (a - 1) + (qb > 0)
                if qb:
                    dve.wait_ge(s["c_row"], 16 * qb)
                elif a == 2:
                    dve.wait_ge(A[1]["c_row"], 16 * NB)
                bad = dve.value_load(flags[0:1, f:f + 1], min_val=0, max_val=P)
                with dve.If(bad != 0):
                    dve.sem_inc(s["gen_f"][qb], 1)
                    with dve.Fori(0, H) as h:
                        for i in range(TB):
                            dve.wait_ge(s["gen_s"][qb], h * TB + i + 1)
                            to = mnat[:, i, bass.ds(h, 1)]
                            if a == 1:
                                at, seen = i * P, (h * TB + i) * 2
                                tt(masked[:, :], ps[:, qb, at:at + P], cmask[:, :], ALU.add)
                                flat = ps[:, :, :].rearrange("p b t -> p (b t)")
                                n = qb * BLK + at
                                if n:
                                    ins = nc.vector.tensor_reduce(mpart[:, 0:1], flat[:, 0:n], AX.X, ALU.max)
                                else:
                                    ins = nc.vector.memset(mpart[:, 0:1], -3e38)
                                mark(ins, s["gen_d"][qb], seen + 1)
                                mark(nc.vector.tensor_reduce(mpart[:, 1:2], masked[:, :], AX.X, ALU.max),
                                     s["gen_d"][qb], seen + 2)
                                tt(to, mpart[:, 0:1], mpart[:, 1:2], ALU.max).then_inc(s["gen_f"][qb], 1)
                            else:
                                nc.vector.tensor_reduce(to, ps[:, 0:4, :], AX.XY, ALU.max).then_inc(s["gen_f"][qb], 1)
                    dve.wait_ge(s["gen_s"][qb], H * TB + 1)
                    mark(ts(negc[:, qb * BLK:(qb + 1) * BLK], ps[0:H, 7, :], -1.0, None, ALU.mult),
                         s["gen_d"][qb], 2 * H * TB + 1 if a == 1 else 1)
                copy(negf[:, :], negc[:, qb * BLK:(qb + 1) * BLK]).then_inc(s["final"], 1)

            def evac(a, done, g):
                s = A[a]
                dve.wait_ge(s["pv"], 2 * (RING + done))
                copy(accs[:, :], sums_bank(g)).then_inc(s["evac"], 1)

            def norm(a, n, g):
                s = A[a]
                dve.wait_ge(s["pt"], n + 1)
                v = sums_bank(g).rearrange("q (p i h c) -> q p i h c", p=2, i=TB, h=2)
                mark(nc.vector.reciprocal(rec[:, :, :, :], v[:, :, :, :, DK]), s["recip"], n + 1)
                for p in range(2):
                    o = att[:, :, (g * HG + 2 * p) * DK:(g * HG + 2 * p + 2) * DK].rearrange("q i (h d) -> q i h d", h=2)
                    ins = tt(o, v[:, p, :, :, 0:DK], rec[:, p].unsqueeze(3).to_broadcast([P, TB, 2, DK]), ALU.mult)
                ins.then_inc(s["norm"], 1)

            def post(a, qb):
                s = A[a]
                dve.wait_ge(s["post_t"], qb + 1)
                copy(attT[:, :], ps6).then_inc(s["post_e"], 1)
                dve.wait_ge(s["post_p"], qb + 1)
                xb = xn[:, qb * TB:(qb + 1) * TB, :]
                if a == 1 and qb == 0:
                    dve.wait_ge(ld_x, 16)
                mark(tt(xb if a == 1 else yb[:, :, :], xb, ps7r, ALU.add), s["post_x"], qb + 1)

            def rows_to_h(b, due):
                xb = xn[:, b * TB:(b + 1) * TB, :]
                link(layernorm(xb, xb))
                due(11)
                y, v, h, t = (nw[:, n, :] for n in (1, 4, 5, 6))
                link(tt(v, y, y, ALU.mult))
                link(tt(v, v, mv[:, :, 1], ALU.mult))
                link(ts(v, v, EPS, None, ALU.add))
                rsqrt(y, v, h, t, 3)
                for i in range(TB):
                    ins = ts(zb[:, i, :], xb[:, i, :], y[:, i:i + 1], None, ALU.mult)
                ins.then_inc(z, 1)

            def split2(b, due):
                s = A[2]
                due(14)
                dve.wait_ge(zT, b + 1)
                ts(hT[:, :], ps6, ln[:, 0:1], ln[:, 1:2], ALU.mult, ALU.add).then_inc(hTs, 1)
                due(16)
                dve.wait_ge(s["k_proj"], b + 1)
                mark(copy(ka[:, :], ps7), s["k_taken"], b + 1)
                if b < NB - 1:
                    dve.wait_ge(s["q_proj"], b + 1)
                    mark(copy(qa[:, :], ps6), s["q_taken"], b + 1)
                if b >= 2:
                    dve.wait_ge(scratch_out, 16 * (2 * NB + 2 * (b - 1)))
                else:
                    dve.wait_ge(scratch_out, 16 * 2 * NB)
                dve.wait_ge(s["nk_mm"] if b else A[1]["nk_mm"], b if b else NB)
                dve.wait_ge(s["nq_mm"] if b else A[1]["nq_mm"], b if b else NB)
                link(copy(k3[:, b % 2, 0, :], ka[:, :]))
                tt(sq[:, 1, :], ka[:, :], ka[:, :], ALU.mult).then_inc(s["sq_k"], 1)
                if b < NB - 1:
                    link(copy(q3[:, b % 2, 0, :], qa[:, :]))
                    mark(tt(sq[:, 0, :], qa[:, :], qa[:, :], ALU.mult), s["sq_q"], b + 1)
                    due(18)
                    dve.wait_ge(s["v_proj"], b + 1)
                    copy(v2[:, b * TB:(b + 1) * TB, :, :], ps6.rearrange("p (i h d) -> p i h d", i=TB, h=H)
                         ).then_inc(s["v_taken"], 1)
                if b == 0:
                    tt(kblk[:, :].rearrange("p (h t) -> p h t", h=H),
                       k3[:, 0, 0, 0:NSUB].unsqueeze(1).to_broadcast([P, H, NSUB]),
                       blk[:, :].unsqueeze(2).to_broadcast([P, H, NSUB]), ALU.mult).then_inc(kbd, 1)
                due(20)
                for work, p3, done in ((ka, k3, "k_split"), (qa, q3, "q_split"))[0:2 if b < NB - 1 else 1]:
                    link(tt(work[:, :], work[:, :], p3[:, b % 2, 0, :], ALU.subtract))
                    link(copy(p3[:, b % 2, 1, :], work[:, :]))
                    tt(p3[:, b % 2, 2, :], work[:, :], p3[:, b % 2, 1, :], ALU.subtract).then_inc(s[done], 1)
                take_key_norms(2, b)
                take_query_norms(2, b)
                for i in range(TB):
                    t = b * TB + i
                    due(21 + i)
                    dve.wait_ge(low_mm, t + 1)
                    mark(nc.vector.tensor_reduce(low[:, t, :], ps[:, low_banks(b, i)[0]:low_banks(b, i)[1] + 1, :].rearrange(
                        "p b (h t) -> p (b h) t", t=NSUB),
                                                 AX.X, ALU.max), low_taken, t + 1)

            def route(b):
                xb = xn[:, b * TB:(b + 1) * TB, :]
                if b:
                    dve.wait_ge(m_done, 16 * b)
                layernorm(zb, yb).then_inc(m_z, 1)
                dve.wait_ge(m_zT, b + 1)
                ts(hT[:, :], ps6, ln[:, 2:3], ln[:, 3:4], ALU.mult, ALU.add).then_inc(m_h, 1)
                link(tt(xb, xb, yb[:, :, :], ALU.add))
                dve.wait_ge(m_g, b + 1)
                link(tt(lg[:, :, :], ps[:, 7, 0:TB * E].rearrange("p (i e) -> p i e", i=TB),
                        gb[:, :].unsqueeze(1).to_broadcast([P, TB, E]), ALU.add))
                for i in range(TB):
                    ins = nc.vector.max(mx8[:, i, :], lg[:, i, :])
                link(ins)
                for i in range(TB):
                    ins = nc.vector.max_index(ix8[:, i, :], mx8[:, i, :], lg[:, i, :])
                link(ins)
                link(copy(ixf[:, :], ix8[:, :, 0]))
                for i in range(TB):
                    ins = ts(oh[:, i, :], iota[:, :], ixf[:, i:i + 1], None, ALU.is_equal)
                ins.then_inc(m_oh, 1)
                dve.wait_ge(m_ohT, b + 1)
                copy(ohT[:, :], ps[0:E, 7, :]).then_inc(m_ohTs, 1)

            def masks(b, e0, e1):
                for e in range(e0, e1):
                    dve.wait_ge(m_mk, b * E + e + 1)
                    mark(copy(ms[:, e, :], ps[:, 6 + e % 2, :]), m_ms, b * E + e + 1)

            def products(b, c):
                for k in range(c * E, (c + 1) * E, 2):
                    n = b * 2 * TB * E + k
                    if n >= PSLOTS:
                        dve.wait_ge(m_mm, n - PSLOTS + 1)
                    tt(prod[:, n % PSLOTS, :], hT[:, :] if c < TB else hid[:, c - TB, :], ms[:, k % E, :], ALU.mult
                       ).then_inc(m_pd, 1)

            def gelu_arg(b, c):
                dve.wait_ge(m_xh, b * TB + c + 1)
                x, t = hid[:, c, :], tg[:, c % 2, :]
                link(tt(t, x, x, ALU.mult))
                link(ts(t, t, 0.044715, 1.0, ALU.mult, ALU.add))
                tt(t, t, x, ALU.mult).then_inc(m_arg, 1)

            def gelu(b, c):
                dve.wait_ge(m_tanh, b * TB + c + 1)
                x, t = hid[:, c, :], tg[:, c % 2, :]
                mark(nc.vector.scalar_tensor_tensor(out=x, in0=t, scalar=1.0, in1=x, op0=ALU.add, op1=ALU.mult),
                     m_hid, b * TB + c + 1)

            def experts(b, due):
                products(b, 0)
                due(19)
                products(b, 1)
                gelu_arg(b, 0)
                products(b, 2)
                gelu(b, 0)
                gelu_arg(b, 1)
                products(b, 3)
                gelu(b, 1)
                gelu_arg(b, 2)
                products(b, TB)
                gelu(b, 2)
                gelu_arg(b, 3)
                products(b, TB + 1)
                gelu(b, 3)
                products(b, TB + 2)
                products(b, TB + 3)
                dve.wait_ge(m_mm, (b + 1) * 2 * TB * E)
                due(32)
                ts(yT[:, :], ps6, 0.5, None, ALU.mult).then_inc(m_yT, 1)

            def finish(b):
                xb = xn[:, b * TB:(b + 1) * TB, :]
                dve.wait_ge(m_yn, b + 1)
                link(tt(xb, xb, ps7r, ALU.add))
                layernorm(zb, xb).then_inc(m_out, 1)

            def attention(a):
                causal = a == 1
                general(a, 0)
                if causal:
                    dve.wait_ge(ld_e, 16 * 11)
                    copy(esel[:, :].rearrange("k (e p) -> k e p", e=E),
                         ident[0:E, 0:E].unsqueeze(2).to_broadcast([E, E, P]))
                for qb in range(NB):
                    base, T = first_step(causal, qb), steps_of(causal, qb)
                    at = [0]

                    def due(step):
                        while at[0] < 2 * G:
                            g, what = divmod(at[0], 2)
                            if step < (g + 1) * T + (TURN_STEP if what else 0):
                                return
                            if what == 0:
                                if g == G - 2 and qb + 1 < NB:
                                    general(a, qb + 1)
                                evac(a, base + (g + 1) * T, g)
                            elif g < G - 1:
                                norm(a, G * qb + g, g)
                            at[0] += 1

                    if qb:
                        norm(a, G * qb - 1, G - 1)
                        due(5)
                        post(a, qb - 1)
                        if causal:
                            rows_to_h(qb - 1, due)
                            split2(qb - 1, due)
                        else:
                            route(qb - 1)
                            masks(qb - 1, 0, 4)
                            due(16)
                            masks(qb - 1, 4, E)
                            experts(qb - 1, due)
                            finish(qb - 1)
                    else:
                        shift(a, 1, NB)
                        for b in range(1, NB):
                            due(SHIFT_AT[b])
                            take_shift(a, b)
                        due(SHIFT_AT[NB])
                        take_ok(a, 2)
                    due(G * T + TURN_STEP)
                norm(a, G * NB - 1, G - 1)
                post(a, NB - 1)

            nc.vector.memset(sums_bank(1), 0.0)
            nc.vector.memset(onesf[:, :], 1.0)
            dve.wait_ge(ld_w, 32)
            copy(blk[:, :], blkf[:, :]).then_inc(init, 1)
            for b in range(NB):
                split1(b)
            take_key_norms(1, NB - 1)
            take_query_norms(1, NB - 1)
            settle(1)
            attention(1)
            b = NB - 1
            at_once = lambda step: None
            rows_to_h(b, at_once)
            split2(b, at_once)
            settle(2)
            attention(2)
            b = NB - 1
            route(b)
            masks(b, 0, E)
            experts(b, at_once)
            finish(b)


def kernel(**inputs):
    import concourse.bacc as _bacc
    from concourse.bass_utils import run_bass_kernel_spmd as _run

    def by_column(w, swapped=False):
        w = np.asarray(w).reshape(D, H, DK // 2, 2)
        return (w[:, :, :, ::-1] if swapped else w).reshape(D, H, DK).transpose(0, 2, 1).reshape(D, D)

    x = inputs["L0_attn_x"].reshape(S, D)
    wq = np.asarray(inputs["L0_attn_q_proj_weight"]).T
    wk = np.asarray(inputs["L0_attn_k_proj_weight"]).T
    wv = np.asarray(inputs["L0_attn_v_proj_weight"]).T
    wqkv = np.asarray(inputs["L0_ffn_w_qkv"])
    inv = (1.0 / THETA ** (np.arange(0, DK, 2, dtype=np.float32) / np.float32(DK))).astype(np.float32)
    ang = np.arange(S, dtype=np.float32)[None, :] * inv[:, None]
    c, s = np.cos(ang).astype(np.float32), np.sin(ang).astype(np.float32)
    cos = np.repeat(np.repeat(c, 2, axis=0), H, axis=0)
    sin = np.repeat(np.stack([-s, s], axis=1).reshape(DK, S), H, axis=0)
    p = np.arange(P)
    given = dict(
        xT=np.asarray(x).T, x=x,
        wa=np.concatenate([by_column(wq), by_column(wq, True), by_column(wk), by_column(wk, True), wv], axis=1),
        wo=np.asarray(inputs["L0_attn_o_proj_weight"]).T,
        wqkv=np.concatenate([by_column(wqkv[:, 0:D]), by_column(wqkv[:, D:2 * D]), wqkv[:, 2 * D:]], axis=1),
        wproj=inputs["L0_ffn_w_proj"],
        ln1w=inputs["L0_ffn_ln1_w"].reshape(D, 1), ln1b=inputs["L0_ffn_ln1_b"].reshape(D, 1),
        ln2w=inputs["L0_ffn_ln2_w"].reshape(D, 1), ln2b=inputs["L0_ffn_ln2_b"].reshape(D, 1),
        gw=inputs["L0_ffn_gate_w"], gb=np.tile(np.asarray(inputs["L0_ffn_gate_b"]).reshape(1, E), (P, 1)),
        w1=inputs["L0_ffn_w1"], w2=inputs["L0_ffn_w2"],
        cos=cos, sin=sin, ident=np.eye(P, dtype=np.float32),
        blk=(p[:, None] % H == np.arange(H)[None, :]).astype(np.float32),
        cmask=np.where(p[None, :] > p[:, None], -3e38, 0.0).astype(np.float32),
        iota=np.tile(np.arange(E, dtype=np.float32), (P, 1)),
        pad=np.repeat(np.array([0] * (SHIFT_ROW - ROWS) + [0x3F803F80], np.uint32)[:, None], PADW, 1).view(np.float32),
    )
    nc = _bacc.Bacc("TRN2", target_bir_lowering=False, num_devices=1)
    arrays, args = {}, []
    for name, a in given.items():
        a = np.ascontiguousarray(a)
        arrays[f"in_{name}"] = a
        args.append(nc.dram_tensor(f"in_{name}", a.shape, mybir.dt.from_np(a.dtype), kind="ExternalInput").ap())
    out = nc.dram_tensor("out_0", (S, D), F32, kind="ExternalOutput").ap()
    build(nc, *args, out)
    r = _run(nc, [arrays], core_ids=[0])
    return r.results[0]["out_0"].reshape(1, S, D)
```
